# Optimizing a Trainium2 kernel written in Bass

```python
import numpy as np
import jax
import jax.numpy as jnp

def _softmax(x, axis=-1):
    return jax.nn.softmax(x, axis=axis)

def _gelu(x):
    return jax.nn.gelu(x, approximate=True)

def _silu(x):
    return jax.nn.silu(x)

def _sigmoid(x):
    return jax.nn.sigmoid(x)

def _layernorm(x, axis=-1, eps=1e-05):
    m = jnp.mean(x, axis=axis, keepdims=True)
    v = jnp.var(x, axis=axis, keepdims=True)
    return (x - m) / jnp.sqrt(v + eps)

def _scatter_add(tgt, idx, src, axis=0):
    return tgt.at[idx].add(src)

def _segment_sum(src, seg, n):
    return jax.ops.segment_sum(src, seg, n)
kernel_name = 'mk_cond_resid_d4_seqx_r2_3b558b'

def setup_inputs(seed: int=0):
    np.random.seed(seed)
    _w = jnp.asarray

    def _rec_inputs():
        import jax
        import jax.numpy as jnp
        _rk = jax.random.key(seed)
        x = -0.0003929 + 0.9999 * jax.random.normal(jax.random.fold_in(_rk, 1), (32, 128, 512), jnp.float32)
        _lenS = 128 - jax.random.randint(jax.random.fold_in(_rk, 7), (32,), 0, max(1, 128 // 4) + 1, jnp.int32)
        _lenS2 = 128 - jax.random.randint(jax.random.fold_in(_rk, 8), (32,), 0, max(1, 128 // 4) + 1, jnp.int32)
        itok_B_0_2 = jax.random.randint(jax.random.fold_in(_rk, 11), (32,), 0, 3, jnp.int32)
        itok_B_0_6 = jax.random.randint(jax.random.fold_in(_rk, 12), (32,), 0, 7, jnp.int32)
        condB_zX = jax.random.uniform(jax.random.fold_in(_rk, 13), (32,), jnp.float32, 0.0, 0.983423)
        condB_zY = jax.random.uniform(jax.random.fold_in(_rk, 14), (32,), jnp.float32, 0.0, 0.979075)
        condB_zR = jax.random.uniform(jax.random.fold_in(_rk, 15), (32,), jnp.float32, 0.0, 0.9968)
        itok_B_0_7 = jax.random.randint(jax.random.fold_in(_rk, 16), (32,), 0, 8, jnp.int32)
        return (x, itok_B_0_2, itok_B_0_6, condB_zX, condB_zY, condB_zR, itok_B_0_7)
    x, itok_B_0_2, itok_B_0_6, condB_zX, condB_zY, condB_zR, itok_B_0_7 = _rec_inputs()

    def _L0_cond_setup():
        import jax, jax.numpy as jnp
        import numpy as np
        NEG_INF = -1e+30
        key = jax.random.key(seed)
        k1, k2, k3, k4, k5 = jax.random.split(key, 5)
        B, S, D, A = (16, 512, 512, 128)
        hidden = jax.random.normal(k1, (B, S, D), dtype=jnp.float32)
        W1 = jax.random.normal(k2, (D, A), dtype=jnp.float32) / np.sqrt(D)
        b1 = jax.random.normal(k3, (A,), dtype=jnp.float32) * 0.01
        v = jax.random.normal(k4, (A,), dtype=jnp.float32) / np.sqrt(A)
        prompt_type_ids = jax.random.randint(k5, (B,), 0, 3, dtype=jnp.int32)
        return {'hidden': hidden, 'W1': W1, 'b1': b1, 'v': v, 'prompt_type_ids': prompt_type_ids}
    _L0_cond_all = _L0_cond_setup()
    _L0_cond_in = {k: v for k, v in _L0_cond_all.items() if k in ('W1', 'b1', 'v')}
    del _L0_cond_all

    def _L1_cond_setup():
        import jax, jax.numpy as jnp
        import numpy as np
        N_PROFILES = 8
        HIDDEN = 512
        BOTTLENECK = 128
        EPS = 1e-05
        key = jax.random.key(seed)
        ks = jax.random.split(key, 8)
        B, S, H, K, P = (16, 1024, HIDDEN, BOTTLENECK, N_PROFILES)
        down_w = jax.random.normal(ks[0], (P, H, K), dtype=jnp.float32) * (1.0 / np.sqrt(H))
        down_b = jax.random.normal(ks[1], (P, K), dtype=jnp.float32) * 0.01
        up_w = jax.random.normal(ks[2], (P, K, H), dtype=jnp.float32) * (1.0 / np.sqrt(K))
        up_b = jax.random.normal(ks[3], (P, H), dtype=jnp.float32) * 0.01
        ln_g = jnp.ones((P, H), dtype=jnp.float32)
        ln_b = jnp.zeros((P, H), dtype=jnp.float32)
        hidden = jax.random.normal(ks[4], (B, S, H), dtype=jnp.float32)
        profile_ids = jax.random.randint(ks[5], (B,), 0, P)
        return {'hidden': hidden, 'profile_ids': profile_ids, 'down_w': down_w, 'down_b': down_b, 'up_w': up_w, 'up_b': up_b, 'ln_g': ln_g, 'ln_b': ln_b}
    _L1_cond_all = _L1_cond_setup()
    _L1_cond_in = {k: v for k, v in _L1_cond_all.items() if k in ('down_w', 'down_b', 'up_w', 'up_b', 'ln_g', 'ln_b')}
    del _L1_cond_all

    def _L2_cond_setup():
        import jax, jax.numpy as jnp
        import numpy as np
        key = jax.random.key(seed)
        k1, k2, k3, k4 = jax.random.split(key, 4)
        B, H, W = (64, 512, 512)
        return {'y': jax.random.uniform(k1, (B, H, W), dtype=jnp.float32), 'zX': jax.random.uniform(k2, (B, 1), dtype=jnp.float32), 'zY': jax.random.uniform(k3, (B, 1), dtype=jnp.float32), 'zR': jax.random.uniform(k4, (B, 1), dtype=jnp.float32), 'dx': 1, 'dy': 1}
    _L2_cond_all = _L2_cond_setup()
    _L2_cond_in = {k: v for k, v in _L2_cond_all.items() if k in ()}
    del _L2_cond_all

    def _L3_cond_setup():
        import jax, jax.numpy as jnp
        import numpy as np
        IN, HID, OUT, PART, E = (512, 2048, 512, 128, 8)
        B, N = (16, 1024)
        key = jax.random.key(seed)
        ks = jax.random.split(key, 8)
        s1 = 1.0 / np.sqrt(IN)
        s2 = 1.0 / np.sqrt(HID)
        return {'x': jax.random.normal(ks[0], (B, N, IN), dtype=jnp.float32), 'indices': jax.random.randint(ks[1], (B,), 0, E, dtype=jnp.int64), 'W1': jax.random.uniform(ks[2], (IN, HID), jnp.float32, -s1, s1), 'b1': jax.random.uniform(ks[3], (HID,), jnp.float32, -s1, s1), 'W2': jax.random.uniform(ks[4], (HID, OUT - PART), jnp.float32, -s2, s2), 'b2': jax.random.uniform(ks[5], (OUT - PART,), jnp.float32, -s2, s2), 'We': jax.random.uniform(ks[6], (E, HID, PART), jnp.float32, -s2, s2), 'be': jax.random.uniform(ks[7], (E, PART), jnp.float32, -s2, s2)}
    _L3_cond_all = _L3_cond_setup()
    _L3_cond_in = {k: v for k, v in _L3_cond_all.items() if k in ('W1', 'b1', 'W2', 'b2', 'We', 'be')}
    del _L3_cond_all
    return {'x': x, 'itok_B_0_2': itok_B_0_2, 'itok_B_0_6': itok_B_0_6, 'condB_zX': condB_zX, 'condB_zY': condB_zY, 'condB_zR': condB_zR, 'itok_B_0_7': itok_B_0_7, 'L0_cond_W1': _L0_cond_in['W1'], 'L0_cond_b1': _L0_cond_in['b1'], 'L0_cond_v': _L0_cond_in['v'], 'L1_cond_down_w': _L1_cond_in['down_w'], 'L1_cond_down_b': _L1_cond_in['down_b'], 'L1_cond_up_w': _L1_cond_in['up_w'], 'L1_cond_up_b': _L1_cond_in['up_b'], 'L1_cond_ln_g': _L1_cond_in['ln_g'], 'L1_cond_ln_b': _L1_cond_in['ln_b'], 'L3_cond_W1': _L3_cond_in['W1'], 'L3_cond_b1': _L3_cond_in['b1'], 'L3_cond_W2': _L3_cond_in['W2'], 'L3_cond_b2': _L3_cond_in['b2'], 'L3_cond_We': _L3_cond_in['We'], 'L3_cond_be': _L3_cond_in['be']}

def reference(x, itok_B_0_2, itok_B_0_6, condB_zX, condB_zY, condB_zR, itok_B_0_7, L0_cond_W1, L0_cond_b1, L0_cond_v, L1_cond_down_w, L1_cond_down_b, L1_cond_up_w, L1_cond_up_b, L1_cond_ln_g, L1_cond_ln_b, L3_cond_W1, L3_cond_b1, L3_cond_W2, L3_cond_b2, L3_cond_We, L3_cond_be):
    import jax
    import jax.numpy as jnp

    def _L0_cond_ref(hidden, W1, b1, v, prompt_type_ids):
        import jax, jax.numpy as jnp
        import numpy as np
        NEG_INF = -1e+30
        B, S, D = hidden.shape
        attn_in = jnp.tanh(jnp.einsum('bsd,da->bsa', hidden, W1) + b1)
        scores = jnp.einsum('bsa,a->bs', attn_in, v)
        idx = jnp.arange(S)
        j = idx[:, None]
        l = idx[None, :]
        prefix_m = l <= j
        postfix_m = l >= j
        cloze_m = l != j
        pt = prompt_type_ids[:, None, None]
        mask = jnp.where(pt == 0, prefix_m[None], jnp.where(pt == 1, postfix_m[None], cloze_m[None]))
        masked_scores = jnp.where(mask, scores[:, None, :], NEG_INF)
        p = jax.nn.softmax(masked_scores, axis=-1)
        cnt = jnp.sum(mask, axis=-1).astype(hidden.dtype)
        pooled = jnp.einsum('bjl,bld->bjd', p, hidden) / cnt[..., None]
        return pooled

    def _L1_cond_ref(hidden, profile_ids, down_w, down_b, up_w, up_b, ln_g, ln_b):
        import jax, jax.numpy as jnp
        import numpy as np
        N_PROFILES = 8
        HIDDEN = 512
        BOTTLENECK = 128
        EPS = 1e-05
        Wd = down_w[profile_ids]
        bd = down_b[profile_ids][:, None]
        Wu = up_w[profile_ids]
        bu = up_b[profile_ids][:, None]
        g = ln_g[profile_ids][:, None]
        b = ln_b[profile_ids][:, None]
        z = jax.nn.relu(jnp.einsum('bsh,bhk->bsk', hidden, Wd) + bd)
        y = hidden + jnp.einsum('bsk,bkh->bsh', z, Wu) + bu
        mu = jnp.mean(y, axis=-1, keepdims=True)
        var = jnp.mean(jnp.square(y - mu), axis=-1, keepdims=True)
        return (y - mu) * jax.lax.rsqrt(var + EPS) * g + b

    def _L2_cond_ref(y, zX, zY, zR, dx, dy):
        import jax, jax.numpy as jnp
        import numpy as np
        yp_x = jnp.pad(y, ((0, 0), (0, 0), (1, 1)), mode='reflect')
        lap_x = (yp_x[:, :, :-2] - 2.0 * y + yp_x[:, :, 2:]) / (dx * dx)
        yp_y = jnp.pad(y, ((0, 0), (1, 1), (0, 0)), mode='reflect')
        lap_y = (yp_y[:, :-2, :] - 2.0 * y + yp_y[:, 2:, :]) / (dy * dy)
        du_dt = zX[:, :, None] * lap_x + zY[:, :, None] * lap_y + zR[:, :, None] * y * (1.0 - y)
        return du_dt

    def _L3_cond_ref(x, indices, W1, b1, W2, b2, We, be):
        import jax, jax.numpy as jnp
        import numpy as np
        IN, HID, OUT, PART, E = (512, 2048, 512, 128, 8)
        B, N = (16, 1024)
        h = jax.nn.gelu(jnp.einsum('bni,ih->bnh', x, W1) + b1, approximate=False)
        shared_x = jnp.einsum('bnh,ho->bno', h, W2) + b2
        We_sel = We[indices]
        be_sel = be[indices]
        expert_x = jnp.einsum('bnh,bhp->bnp', h, We_sel) + be_sel[:, None, :]
        return jnp.concatenate([shared_x, expert_x], axis=-1)
    x = x + _L0_cond_ref(x, L0_cond_W1, L0_cond_b1, L0_cond_v, itok_B_0_2)
    x = x + _L1_cond_ref(x, itok_B_0_6, L1_cond_down_w, L1_cond_down_b, L1_cond_up_w, L1_cond_up_b, L1_cond_ln_g, L1_cond_ln_b)
    x = x + _L2_cond_ref(x, condB_zX[:, None], condB_zY[:, None], condB_zR[:, None], 1, 1)
    x = x + _L3_cond_ref(x, itok_B_0_7, L3_cond_W1, L3_cond_b1, L3_cond_W2, L3_cond_b2, L3_cond_We, L3_cond_be)
    return x

_drawn_inputs = setup_inputs


def setup_inputs(seed=0):
    import zlib

    import numpy as np

    out = dict(_drawn_inputs(seed))
    spreads = {'L1_cond_ln_g': (1.0, 0.2), 'L1_cond_ln_b': (0.0, 0.1)}
    factors = {'L0_cond_W1': 5.091,
     'L0_cond_b1': 64.0,
     'L0_cond_v': 4.004,
     'L1_cond_down_b': 8.0,
     'L1_cond_up_b': 8.0,
     'L3_cond_b1': 27.534,
     'L3_cond_b2': 24.21,
     'L3_cond_be': 44.688}
    for name, (base, spread) in spreads.items():
        noise = np.random.default_rng([zlib.crc32(name.encode()), seed]).standard_normal(out[name].shape)
        drawn = base * np.exp(spread * noise) if base else spread * noise
        out[name] = jnp.asarray(drawn.astype(out[name].dtype))
    for name, factor in factors.items():
        out[name] = (out[name] * factor).astype(out[name].dtype)
    return out
```

```python
from contextlib import ExitStack

import concourse.bass as bass
from concourse import mybir

F32 = mybir.dt.float32
F32R = mybir.dt.float32r
I32 = mybir.dt.int32
BF16 = mybir.dt.bfloat16
ALU = mybir.AluOpType
ACT = mybir.ActivationFunctionType
AX = mybir.AxisListType

P = 128
NSEQ = 32
D = 512
DC = D // P
NPAIR = NSEQ // 2
TOK = 2 * P
HID = 2048
HC = HID // P
SH = 384
EX = 128
NPROF = 8
NEXP = 8
NEG = -1e30
EPS = 1e-5
W2C = EX + SH + EX
EPER = HC // 2
STEADY = dict(pen=0, hid=0, score=1, split_x=(3, 5), pt=(3, 5), pool=(4, 6), turn=(5, 7), down=(6, 9), up=(7, 10),
              norm=(8, 11), x2=(9, 12), hi2=(10, 13), lo2=(11, 13), lap=(12, 14), split_xT=13, load_bias=(5, 9),
              load_down=(6, 9), load_up=(6, 9), load_gain=(8, 11), load_xT=9, load_x=13)
OPENING = dict(pen=0, hid=0, score=1, split_x=(0, 1), pt=(2, 3), pool=(4, 5), turn=(5, 6), down=(7, 10), up=(9, 12),
               norm=(11, 14), x2=(13, 16), hi2=(14, 17), lo2=(14, 17), lap=(15, 19), load_bias=(7, 13),
               load_down=(10, 14), load_up=(10, 14), load_gain=(14, 19), load_xT=15, load_x=22)
OPENING_SLOTS = 26
RES_AT = 3
SPLIT_L0_AT = 12
LOAD_EXPERTS, SPLIT_EXPERTS = 3, 6
EARLY_LOAD = {7: 2, 12: 3, 17: 4}
EARLY_AT = {8: 0, 12: 1, 15: 2, 17: 3, 19: 4}
LATE_LOAD = {0: 5, 3: 6, 6: 7}
LATE_AT = {0: 5, 1: 6, 2: 7, 3: 8, 4: 9, 5: 10, 6: 11, 7: 12, 8: 13, 9: 14, 10: 15}


def experts_at(t, offset):
    if (t - offset) % 2:
        return None
    c = (t - offset) // 2
    return (1, c) if c >= 0 else (0, c + EPER)


def need(eng, sem, n):
    if isinstance(n, int) and n <= 0:
        return
    eng.wait_ge(sem, n)


def build(nc, x, xT, pt, prof, zXYR, expert, l0_w1, cols_in, dw, db, uw, ub, lng, lnb,
          w1, w2, b2, we, be, out):
    with ExitStack() as ctx:
        def sb(name, shape, dt=F32):
            return ctx.enter_context(nc.sbuf_tensor(name, shape, dt))

        def psum(name, shape):
            return ctx.enter_context(nc.psum_tensor(name, shape, F32))

        def sem(name):
            return ctx.enter_context(nc.semaphore(name))

        shapes = dict(w1=[P, DC, HID], w2e=[P, HC, W2C], l0_w1=[P, DC, P], xT=[P, DC * TOK])
        with ExitStack() as loaded:
            w1_raw, w2e_raw, l0_w1_raw, xT_raw = (loaded.enter_context(nc.sbuf_tensor(f"{n}_raw", shape, F32))
                                                  for n, shape in shapes.items())
        w1_lo, w2e_lo, l0_w1_lo, xT_lo = (sb(f"{n}_lo", shape, F32R) for n, shape in shapes.items())
        w1_hi, w2e_hi, l0_w1_hi = (sb(f"{n}_hi", shapes[n], F32R) for n in ("w1", "w2e", "l0_w1"))
        res = sb("res", [P, 2, D])
        x3T_hi = sb("x3T_hi", [P, DC, TOK], F32R)
        x3T_lo = sb("x3T_lo", [P, DC, TOK], F32R)
        h_hi = sb("h_hi", [P, 2, TOK], F32R)
        h_lo = sb("h_lo", [P, 2, TOK], F32R)
        x3 = sb("x3", [P, 2, D])
        xT_v = xT_raw[:, :].rearrange("p (c n) -> p c n", c=DC)
        x1T_v = xT_raw[:, :].rearrange("p (j c n) -> p j c n", j=2, c=DC)
        xT_lo = xT_lo[:, :].rearrange("p (c n) -> p c n", c=DC)
        xt = sb("xt", [P, 2, D])
        ya = sb("ya", [P, 2, D])
        scratch = [sb("scratch0", [P, 2 * D], F32R), sb("scratch1", [P, 2 * D], F32R)]
        wide_hi, wide_lo = [a[:, 0:D] for a in scratch], [a[:, D:2 * D] for a in scratch]
        xT_hi = scratch[0][:, :].rearrange("p (c n) -> p c n", c=DC)
        side_hi = sb("side_hi", [P, P], F32R)
        side_lo = sb("side_lo", [P, P], F32R)
        dw_sb = sb("dw_sb", [P, DC, P])
        uw_sb = sb("uw_sb", [P, D])

        def adapter(k):
            if isinstance(k, int) and k == 1:
                return res[:, 0, :].rearrange("p (c n) -> p c n", c=DC), res[:, 1, :]
            return dw_sb[:, :, :], uw_sb[:, :]

        db_sb = sb("db_sb", [P, 1])
        ub_sb = sb("ub_sb", [P, D])
        lng_sb = sb("lng_sb", [P, D])
        lnb_sb = sb("lnb_sb", [P, D])
        be_sb = sb("be_sb", [P, 2, EX])
        b2_sb = sb("b2_sb", [P, SH])
        th = sb("th", [P, TOK])
        prob = sb("prob", [P, 2, P])
        vrep = sb("vrep", [P, P])
        ident = sb("ident", [P, P])
        after = sb("after", [P, P], BF16)
        before = sb("before", [P, P], BF16)
        lap = sb("lap", [P, P], F32R)
        cols = sb("cols", [P, HC + 2])
        b1_sb, l0_b1_sb, l0_v_sb = cols[:, 0:HC], cols[:, HC:HC + 1], cols[:, HC + 1:HC + 2]
        idx = sb("idx", [1, 2, NSEQ], I32)
        pt_i = sb("pt_i", [P, NSEQ], I32)
        zxyr = sb("zxyr", [P, 3, NSEQ])
        zx, zy, zr = (zxyr[:, i, :] for i in range(3))
        nzr = sb("nzr", [P, NSEQ])
        qb = sb("qb", [P, NSEQ])
        cp = sb("cp", [P, 3, NSEQ])
        cnt = sb("cnt", [P, NSEQ])
        rows = sb("rows", [P, 2])
        half = sb("half", [P, 1])
        nmax = sb("nmax", [P, 2])
        esum = sb("esum", [P, 2])
        den = sb("den", [P, 2])
        rden = sb("rden", [P, 2])
        stats = sb("stats", [P, 6])
        mv = sb("mv", [P, 2])
        vpe = sb("vpe", [P, 1])
        warm = sb("warm", [P, 1])
        rstd = sb("rstd", [P, 1])

        acc = [psum("acc0", [P, D]), psum("acc1", [P, D])]
        h_ps = [psum("h_ps0", [P, D]), psum("h_ps1", [P, D])]
        sc = psum("sc", [P, 2, TOK])
        small = psum("small", [P, 4, P])
        turn = psum("turn", [P, DC, P])
        wide = psum("wide", [P, D])
        turned = [turn[:, :, :], wide[:, :].rearrange("p (c n) -> p c n", c=DC)]

        def h_slot(t):
            return h_ps[t % 2][:, 0:TOK]


        l0_in, par_in, b2_in = sem("l0_in"), sem("par_in"), sem("b2_in")
        idx_in = sem("idx_in")
        masks_made = sem("masks_made")
        tab = sem("tab")
        w_in = [sem(f"w_in{g}") for g in range(HC // 2)]
        w1_hi_made, w1_lo_made = sem("w1_hi_made"), sem("w1_lo_made")
        w2_hi_made, w2_lo_made = sem("w2_hi_made"), sem("w2_lo_made")
        e_hi_made, e_lo_made = sem("e_hi_made"), sem("e_lo_made")
        xT_in, x_in = sem("xT_in"), sem("x_in")
        dw_in, uw_in = [sem("dw_in0"), sem("dw_in1")], [sem("uw_in0"), sem("uw_in1")]
        db_in = sem("db_in")
        ub_in, lnb_in, lng_in = sem("ub_in"), sem("lnb_in"), sem("lng_in")
        be_in = sem("be_in")
        hid_done, th_made, sc_done = sem("hid_done"), sem("th_made"), sem("sc_done")
        pen_made, ms_made, nmax_made = sem("pen_made"), sem("ms_made"), sem("nmax_made")
        exp_made, den_made, rden_made = sem("exp_made"), sem("den_made"), sem("rden_made")
        pT_done, pool_done, x1_made = sem("pT_done"), sem("pool_done"), sem("x1_made")
        wide_hi_made = [sem("wide_hi_made0"), sem("wide_hi_made1")]
        wide_lo_made = [sem("wide_lo_made0"), sem("wide_lo_made1")]
        side_hi_made, side_lo_made = sem("side_hi_made"), sem("side_lo_made")
        xb_made = sem("xb_made")
        x1T_done, x1T_made = sem("x1T_done"), sem("x1T_made")
        xT_hi_made, xT_lo_made = sem("xT_hi_made"), sem("xT_lo_made")
        l0_hi_made, l0_lo_made = sem("l0_hi_made"), sem("l0_lo_made")
        down_done, z_made, up_done = sem("down_done"), sem("z_made"), sem("up_done")
        y_made, stats_made, mv_made = sem("y_made"), sem("stats_made"), sem("mv_made")
        eps_set, vpe_made, rstd_made = sem("eps_set"), sem("vpe_made"), sem("rstd_made")
        norm_made, scaled_made = sem("norm_made"), sem("scaled_made")
        x2_made, edge_made = sem("x2_made"), sem("edge_made")
        nb_made, q_made, u_made = sem("nb_made"), sem("q_made"), sem("u_made")
        v_made, lap_done, x3_made = sem("v_made"), sem("lap_done"), sem("x3_made")
        x3T_done, x3T_hi_made, x3T_lo_made = sem("x3T_done"), sem("x3T_hi_made"), sem("x3T_lo_made")
        h_done, gelu_made = sem("h_done"), sem("gelu_made")
        h_hi_made, h_lo_made = sem("h_hi_made"), sem("h_lo_made")
        out_done = sem("out_done")
        res_made, sum_made, stored = sem("res_made"), sem("sum_made"), sem("stored")

        block = ctx.enter_context(nc.Block())

        @block.sync
        def _(sp):
            def index(row, k):
                return nc.sync.value_load(idx[0:1, row, bass.ds(k, 1)], min_val=0, max_val=7)

            def load_xT(s):
                need(sp, down_done, 2 * s)
                sp.dma_start(xT_v, xT[:, bass.ds(s * TOK, TOK)].rearrange("(c p) n -> p c n", p=P)).then_inc(xT_in, 16)

            def load_x(s):
                for j in range(2):
                    need(sp, wide_lo_made[j], 3 * s)
                need(sp, u_made, 2 * s)
                need(sp, nb_made, 2 * s)
                sp.dma_start(xt[:, :, :], x[bass.ds(2 * s, 2)].rearrange("j p n -> p j n")).then_inc(x_in, 16)

            def load_down(e, j, k):
                need(sp, z_made, k)
                if not (isinstance(k, int) and k == 1):
                    load_down_weights(e, j, k)
                sp.dma_start(db_sb[:, :], db[bass.ds(e, 1)].rearrange("a (p o) -> p (a o)", o=1)).then_inc(db_in, 16)

            def load_down_weights(e, j, k):
                sp.dma_start(adapter(k)[0], dw[bass.ds(e, 1)].rearrange("a (c p) n -> p (a c) n", p=P)).then_inc(dw_in[j], 16)

            def load_up_weights(e, j, k):
                sp.dma_start(adapter(k)[1], uw[bass.ds(e, 1)].rearrange("a p n -> p (a n)")).then_inc(uw_in[j], 16)

            def load_up(e, j, split_before):
                need(sp, wide_lo_made[1 - j], split_before)
                load_up_weights(e, j, None)

            def every(src, e):
                return src[bass.ds(e, 1)].rearrange("a n -> (a n)").partition_broadcast(P)

            def load_biases(e, k):
                need(sp, xb_made, 2 * k)
                sp.dma_start(ub_sb[:, :], every(ub, e)).then_inc(ub_in, 16)
                sp.dma_start(lnb_sb[:, :], every(lnb, e)).then_inc(lnb_in, 16)

            def load_gain(e, k):
                need(sp, scaled_made, k)
                sp.dma_start(lng_sb[:, :], every(lng, e)).then_inc(lng_in, 16)

            def load_expert_bias(es, p):
                need(sp, res_made, 4 * p)
                for j in range(2):
                    sp.dma_start(be_sb[:, j, :], every(be, es[j])).then_inc(be_in, 16)

            def load_weights(g, es):
                two, rows_ = slice(2 * g, 2 * g + 2), slice(2 * g * P, 2 * (g + 1) * P)
                sp.dma_start(w1_raw[:, :, rows_], w1[:, rows_].rearrange("(c p) n -> p c n", p=P)).then_inc(w_in[g], 16)
                sp.dma_start(w2e_raw[:, two, EX:EX + SH],
                             w2[rows_, :].rearrange("(h p) n -> p h n", p=P)).then_inc(w_in[g], 16)
                for j in range(2):
                    load_expert(g, j, es[j], w_in[g])

            def load_expert(c, j, e, landed):
                at = j * (EX + SH)
                sp.dma_start(w2e_raw[:, 2 * c:2 * c + 2, at:at + EX],
                             we[bass.ds(e, 1), 2 * c * P:2 * (c + 1) * P, :].rearrange(
                                 "a (h p) n -> p (a h) n", p=P)).then_inc(landed, 16)

            def load_experts(p, c, es):
                sp.wait_ge(out_done, HC * (p - 1) + 2 * c + 2)
                for j in range(2):
                    load_expert(c, j, es[j], w_in[c])

            def store(p):
                for j in range(2):
                    sp.wait_ge(sum_made, 4 * p + 2 * j + 2)
                    sp.dma_start(out[bass.ds(2 * p + j, 1)].rearrange("a p n -> p (a n)"), res[:, j, :]).then_inc(stored, 16)

            def step(p, front, mlp):
                s = p + 1
                at = STEADY if mlp else OPENING
                more = front and not (isinstance(s, int) and s == NPAIR - 1)
                if mlp:
                    es = [index(1, 2 * p + j) for j in range(2)]
                if mlp and front:
                    es_next = [index(1, 2 * s + j) for j in range(2)]
                if front:
                    e1 = index(0, 2 * s + 1)
                if more:
                    e2 = index(0, 2 * s + 2)
                first = isinstance(p, int) and p == 0
                for t in range(HC if mlp else OPENING_SLOTS):
                    if mlp and t == 1 and not first:
                        store(p - 1)
                    if mlp and experts_at(t, LOAD_EXPERTS):
                        ahead, c = experts_at(t, LOAD_EXPERTS)
                        if (ahead and front) or not (ahead or first):
                            load_experts(p + ahead, c, es_next if ahead else es)
                    if mlp and front and t == 4:
                        load_expert_bias(es_next, s)
                    if front and t == at["load_bias"][0]:
                        load_biases(e1, 2 * s + 1)
                    if front and t == at["load_down"][0]:
                        load_down(e1, 1, 2 * s + 1)
                    if front and mlp and t == at["load_up"][0]:
                        load_up(e1, 1, 3 * s + 2)
                    if front and t == at["load_gain"][0]:
                        load_gain(e1, 2 * s + 1)
                    if more and t == at["load_xT"]:
                        load_xT(s + 1)
                    if more and t == at["load_down"][1]:
                        load_down(e2, 0, 2 * s + 2)
                    if more and t == at["load_up"][1]:
                        load_up(e2, 0, 3 * s + 2)
                    if more and t == at["load_bias"][1]:
                        load_biases(e2, 2 * s + 2)
                    if more and t == at["load_gain"][1]:
                        load_gain(e2, 2 * s + 2)
                    if more and t == at["load_x"]:
                        load_x(s + 1)
                    if front and not mlp and t in EARLY_LOAD:
                        load_weights(EARLY_LOAD[t], es_first)
                    if first and t in LATE_LOAD:
                        load_weights(LATE_LOAD[t], es)

            load_xT(0)
            sp.dma_start(l0_w1_raw[:, :, :], l0_w1.rearrange("(c p) n -> p c n", p=P)).then_inc(l0_in, 16)
            sp.dma_start(cols[:, :], cols_in).then_inc(l0_in, 16)
            sp.dma_start(pt_i[:, :], pt.rearrange("a n -> (a n)").partition_broadcast(P)).then_inc(par_in, 16)
            sp.dma_start(idx[:, 0, :], prof).then_inc(idx_in, 16)
            sp.dma_start(idx[:, 1, :], expert).then_inc(idx_in, 16)
            load_x(0)
            sp.dma_start(zxyr[:, :, :].rearrange("p a n -> p (a n)"),
                         zXYR.rearrange("a n -> (a n)").partition_broadcast(P)).then_inc(par_in, 16)
            sp.wait_ge(idx_in, 32)
            e_first = index(0, 0)
            es_first = [index(1, j) for j in range(2)]
            load_biases(e_first, 0)
            load_down(e_first, 0, 0)
            load_up(e_first, 0, 0)
            e_second = index(0, 1)
            load_weights(0, es_first)
            load_down_weights(e_second, 1, 1)
            load_up_weights(e_second, 1, 1)
            load_gain(e_first, 0)
            load_weights(1, es_first)
            sp.dma_start(b2_sb[:, :], b2.rearrange("a n -> (a n)").partition_broadcast(P)).then_inc(b2_in, 16)
            load_expert_bias(es_first, 0)
            step(-1, True, False)
            step(0, True, True)
            with nc.sync.Fori(1, NPAIR - 2) as p:
                step(p, True, True)
            step(NPAIR - 2, True, True)
            step(NPAIR - 1, False, True)
            store(NPAIR - 1)
            sp.wait_ge(stored, 32 * NPAIR)

        @block.gpsimd
        def _(pool):
            def fill(tile, value):
                pool.memset(tile, value).then_inc(masks_made, 1)

            fill(ident[:, :], 0.0)
            fill(after[:, :], 0.0)
            fill(before[:, :], 0.0)
            lap_raw = ya[:, 0, 0:P]
            fill(lap_raw, 0.0)
            fill(half[:, :], -0.5)
            pool.wait_ge(masks_made, 5)

            def mark(tile, value, base, step_p, step_f, op, n=P):
                pool.affine_select(out=tile, in_=tile, compare_op=op, fill=value, base=base,
                                   pattern=[[step_f, n]], channel_multiplier=step_p).then_inc(masks_made, 1)

            mark(ident[:, :], 1.0, 0, 1, -1, ALU.not_equal)
            mark(after[:, :], 1.0, 0, 1, -1, ALU.is_ge)
            mark(before[:, :], 1.0, 0, -1, 1, ALU.is_ge)
            mark(lap_raw, -2.0, 0, 1, -1, ALU.not_equal)
            pool.wait_ge(masks_made, 9)
            mark(lap_raw, 1.0, -1, 1, -1, ALU.not_equal)
            pool.wait_ge(masks_made, 10)
            mark(lap_raw, 1.0, 1, 1, -1, ALU.not_equal)
            pool.wait_ge(masks_made, 11)
            mark(lap_raw[:, 0:1], 2.0, -1, 1, 0, ALU.not_equal, 1)
            mark(lap_raw[:, P - 1:P], 2.0, -(P - 2), 1, 0, ALU.not_equal, 1)
            pool.wait_ge(masks_made, 13)
            pool.tensor_copy(lap[:, :], lap_raw).then_inc(masks_made, 1)

            def split_w2_lo(w):
                pool.wait_ge(w2_hi_made, w + 1)
                pool.tensor_tensor(w2e_lo[:, w, :], w2e_raw[:, w, :], w2e_hi[:, w, :].bitcast(F32),
                                   ALU.subtract).then_inc(w2_lo_made, 1)

            def step(p, front, mlp):
                s = p + 1
                at = STEADY if mlp else OPENING
                first = isinstance(p, int) and p == 0
                for t in range(HC if mlp else OPENING_SLOTS):
                    if mlp and t == RES_AT:
                        need(pool, stored, 32 * p)
                        need(pool, x3_made, 2 * (p + 1))
                        need(pool, be_in, 32 * (p + 1))
                        if isinstance(p, int) and p == 0:
                            pool.wait_ge(b2_in, 16)
                        for j in range(2):
                            pool.tensor_tensor(res[:, j, 0:SH], x3[:, j, 0:SH], b2_sb[:, :], ALU.add).then_inc(res_made, 1)
                            pool.tensor_tensor(res[:, j, SH:D], x3[:, j, SH:D], be_sb[:, j, :], ALU.add).then_inc(res_made, 1)
                    for j in range(2 if front else 0):
                        k = 2 * s + j
                        if t == at["pool"][j]:
                            need(pool, x1_made, k + 1)
                            need(pool, v_made, k - 1)
                            need(pool, ub_in, 16 * (k + 1))
                            pool.tensor_tensor(ya[:, j, :], xt[:, j, :], ub_sb[:, :], ALU.add).then_inc(xb_made, 1)
                            need(pool, lnb_in, 16 * (k + 1))
                            need(pool, x3T_done, 2 * s)
                            need(pool, res_made, 4 * s)
                            pool.tensor_tensor(x3[:, j, :], xt[:, j, :], lnb_sb[:, :], ALU.add).then_inc(xb_made, 1)
                        if t == at["up"][j]:
                            need(pool, vpe_made, k + 1)
                            pool.tensor_tensor(rstd[:, :], vpe[:, :], half[:, :], ALU.pow).then_inc(rstd_made, 1)
                        if t == at["x2"][j]:
                            need(pool, x2_made, k + 1)
                            pool.tensor_tensor(ya[:, j, 1:D - 1], xt[:, j, 0:D - 2], xt[:, j, 2:D], ALU.add).then_inc(nb_made, 1)
                    if front and not mlp and t in EARLY_AT:
                        split_w2_lo(EARLY_AT[t])
                    if first and t in LATE_AT:
                        split_w2_lo(LATE_AT[t])

            step(-1, True, False)
            step(0, True, True)
            with nc.gpsimd.Fori(1, NPAIR - 1) as p:
                step(p, True, True)
            step(NPAIR - 1, False, True)

        @block.scalar
        def _(act):
            def split_weights_hi(w):
                act.wait_ge(w_in[w // 2], 64)
                act.copy(w1_hi[:, :, w * P:(w + 1) * P], w1_raw[:, :, w * P:(w + 1) * P]).then_inc(w1_hi_made, 1)
                act.copy(w2e_hi[:, w, :], w2e_raw[:, w, :]).then_inc(w2_hi_made, 1)

            def split_experts_hi(p, c):
                act.wait_ge(w_in[c], 64 + 32 * p)
                act.copy(experts_of(w2e_hi, c), experts_of(w2e_raw, c)).then_inc(e_hi_made, 1)

            def step(p, front, mlp):
                s = p + 1
                at = STEADY if mlp else OPENING
                more = front and not (isinstance(s, int) and s == NPAIR - 1)
                first = isinstance(p, int) and p == 0
                for t in range(HC if mlp else OPENING_SLOTS):
                    if mlp:
                        n = HC * p + t
                        act.wait_ge(h_done, n + 1)
                        act.activation(h_slot(t), h_slot(t), ACT.Gelu, bias=b1_sb[:, t:t + 1]).then_inc(gelu_made, 1)
                    if first and t == SPLIT_L0_AT:
                        act.copy(l0_w1_hi[:, :, :], l0_w1_raw[:, :, :]).then_inc(l0_hi_made, 1)
                    if front and t == at["hid"]:
                        need(act, hid_done, s + 1)
                        need(act, sc_done, s)
                        act.activation(th[:, :], sc[:, 0, :], ACT.Tanh, bias=l0_b1_sb[:, 0:1]).then_inc(th_made, 1)
                    if front and t == at["score"]:
                        need(act, nmax_made, s + 1)
                        for j in range(2):
                            act.activation(prob[:, j, :], prob[:, j, :], ACT.Exp, bias=nmax[:, j:j + 1],
                                           accum_out=esum[:, j:j + 1]).then_inc(exp_made, 1)
                    for j in range(2 if front else 0):
                        k = 2 * s + j
                        if t == at["split_x"][j]:
                            need(act, x_in, 16 * (s + 1))
                            need(act, lap_done, k - 1)
                            act.copy(wide_hi[j], xt[:, j, :]).then_inc(wide_hi_made[j], 1)
                        if t == at["pt"][j]:
                            if j == 0:
                                need(act, up_done, k)
                            else:
                                need(act, pool_done, k)
                            need(act, pT_done, k + 1)
                            act.copy(side_hi[:, :], small[:, 0, :]).then_inc(side_hi_made, 1)
                        if t == at["turn"][j]:
                            need(act, x1T_done, k + 1)
                            act.copy(x1T_v[:, j, :, :], turn[:, :, :]).then_inc(x1T_made, 1)
                        if t == at["down"][j]:
                            need(act, uw_in[j], 16 * (s + 1))
                            need(act, pool_done, k + 1)
                            act.copy(wide_hi[j], adapter(k)[1]).then_inc(wide_hi_made[j], 1)
                            need(act, down_done, k + 1)
                            need(act, db_in, 16 * (k + 1))
                            act.activation(small[:, 1, :], small[:, 1, :], ACT.Relu, bias=db_sb[:, 0:1]).then_inc(z_made, 1)
                            need(act, z_made, k + 1)
                            if j == 0:
                                need(act, pool_done, k + 2)
                            else:
                                need(act, up_done, k)
                            act.copy(side_hi[:, :], small[:, 1, :]).then_inc(side_hi_made, 1)
                        if t == at["hi2"][j]:
                            need(act, x2_made, k + 1)
                            need(act, up_done, k + 1)
                            act.copy(wide_hi[j], xt[:, j, :]).then_inc(wide_hi_made[j], 1)
                            if isinstance(k, int) and k == 0:
                                act.wait_ge(tab, TAB_OPS)
                            act.activation(x3[:, j, :], xt[:, j, :], ACT.Identity, bias=qb[:, bass.ds(k, 1)],
                                           scale=nzr[:, bass.ds(k, 1)]).then_inc(q_made, 1)
                    if mlp and more and t == at["split_xT"]:
                        need(act, lap_done, 2 * s + 1)
                        need(act, xT_in, 16 * (s + 2))
                        act.copy(xT_hi, xT_v).then_inc(xT_hi_made, 1)
                    if front and not mlp and t in EARLY_AT:
                        split_weights_hi(EARLY_AT[t])
                    if first and t in LATE_AT:
                        split_weights_hi(LATE_AT[t])
                    if mlp and experts_at(t, SPLIT_EXPERTS):
                        ahead, c = experts_at(t, SPLIT_EXPERTS)
                        if (ahead and front) or not (ahead or first):
                            split_experts_hi(p + ahead, c)
                for j in range(2 if front else 0):
                    need(act, x3T_done, 2 * s + j + 1)
                    act.copy(x3T_hi[:, :, j * P:(j + 1) * P], turned[j]).then_inc(x3T_hi_made, 1)

            act.wait_ge(masks_made, 5)
            act.activation(warm[:, :], half[:, :], ACT.Tanh)
            act.wait_ge(l0_in, 32)
            step(-1, True, False)
            step(0, True, True)
            with nc.scalar.Fori(1, NPAIR - 2) as p:
                step(p, True, True)
            step(NPAIR - 2, True, True)
            step(NPAIR - 1, False, True)

        @block.vector
        def _(dve):
            made = [0]

            def table(ins):
                made[0] += 1
                ins.then_inc(tab, 1)
                dve.wait_ge(tab, made[0])

            def setup():
                dve.wait_ge(l0_in, 32)
                table(dve.memset(vrep[:, :], 1.0))
                table(dve.tensor_scalar(vrep[:, :], vrep[:, :], l0_v_sb[:, 0:1], None, ALU.mult))
                dve.wait_ge(masks_made, MASK_OPS)
                table(dve.tensor_reduce(rows[:, 0:1], after[:, :], AX.X, ALU.add))
                table(dve.tensor_reduce(rows[:, 1:2], before[:, :], AX.X, ALU.add))
                table(dve.tensor_scalar(rows[:, :], rows[:, :], -1.0, float(P), ALU.mult, ALU.add))
                dve.wait_ge(par_in, 32)
                table(dve.tensor_copy(cnt[:, :], pt_i[:, :]))
                table(dve.tensor_scalar(cp[:, 0, :], cnt[:, :], 0.0, NEG, ALU.is_equal, ALU.mult))
                table(dve.tensor_scalar(cp[:, 1, :], cnt[:, :], 1.0, NEG, ALU.is_equal, ALU.mult))
                table(dve.tensor_tensor(cp[:, 2, :], cp[:, 0, :], cp[:, 1, :], ALU.add))
                table(dve.tensor_scalar(cp[:, 2, :], cp[:, 2, :], -1.0, NEG, ALU.mult, ALU.add))

            def setup_counts():
                table(dve.tensor_scalar(nzr[:, :], cnt[:, :], 0.0, None, ALU.is_equal))
                table(dve.tensor_scalar(qb[:, :], cnt[:, :], 1.0, None, ALU.is_equal))
                table(dve.tensor_tensor(cnt[:, :], nzr[:, :], qb[:, :], ALU.add))
                table(dve.tensor_scalar(cnt[:, :], cnt[:, :], -float(P - 1), float(P - 1), ALU.mult, ALU.add))
                table(dve.scalar_tensor_tensor(cnt[:, :], nzr[:, :], rows[:, 0:1], cnt[:, :], ALU.mult, ALU.add))
                table(dve.scalar_tensor_tensor(cnt[:, :], qb[:, :], rows[:, 1:2], cnt[:, :], ALU.mult, ALU.add))

            def setup_stencil():
                table(dve.tensor_scalar(nzr[:, :], zr, -1.0, None, ALU.mult))
                table(dve.tensor_scalar(qb[:, :], zr, 1.0, None, ALU.add))
                table(dve.scalar_tensor_tensor(qb[:, :], zx, -2.0, qb[:, :], ALU.mult, ALU.add))

            def split_w1_lo(w):
                part = slice(w * P, (w + 1) * P)
                dve.wait_ge(w1_hi_made, w + 1)
                dve.tensor_tensor(w1_lo[:, :, part], w1_raw[:, :, part], w1_hi[:, :, part].bitcast(F32),
                                  ALU.subtract).then_inc(w1_lo_made, 1)

            def split_wide_lo(source, j, w):
                need(dve, wide_hi_made[j], w + 1)
                dve.tensor_tensor(wide_lo[j], source, wide_hi[j].bitcast(F32), ALU.subtract).then_inc(wide_lo_made[j], 1)

            def split_side_lo(source, v):
                need(dve, side_hi_made, v + 1)
                dve.tensor_tensor(side_lo[:, :], source, side_hi[:, :].bitcast(F32), ALU.subtract).then_inc(side_lo_made, 1)

            def split_experts_lo(p, c):
                dve.wait_ge(e_hi_made, EPER * (p - 1) + c + 1)
                dve.tensor_tensor(experts_of(w2e_lo, c), experts_of(w2e_raw, c),
                                  experts_of(w2e_hi, c).bitcast(F32), ALU.subtract).then_inc(e_lo_made, 1)

            def add_residual(p):
                dve.wait_ge(out_done, HC * (p + 1))
                need(dve, res_made, 4 * (p + 1))
                for j, cols, at in ((0, slice(0, SH), EX), (0, slice(SH, D), 0), (1, slice(0, SH), 0), (1, slice(SH, D), SH)):
                    dve.tensor_tensor(res[:, j, cols], acc[j][:, at:at + cols.stop - cols.start], res[:, j, cols],
                                      ALU.add).then_inc(sum_made, 1)

            def step(p, front, mlp):
                s = p + 1
                at = STEADY if mlp else OPENING
                more = front and not (isinstance(s, int) and s == NPAIR - 1)
                first = isinstance(p, int) and p == 0
                for t in range(HC if mlp else OPENING_SLOTS):
                    if mlp and t == 0 and not first:
                        add_residual(p - 1)
                    if first and t == SPLIT_L0_AT:
                        dve.wait_ge(l0_hi_made, 1)
                        dve.wait_ge(hid_done, 2)
                        dve.tensor_tensor(l0_w1_lo[:, :, :], l0_w1_raw[:, :, :], l0_w1_hi[:, :, :].bitcast(F32),
                                          ALU.subtract).then_inc(l0_lo_made, 1)
                    if front and t == at["pen"]:
                        need(dve, pT_done, 2 * s)
                        for j in range(2):
                            k = 2 * s + j
                            dve.tensor_scalar(prob[:, j, :], after[:, :], cp[:, 0, bass.ds(k, 1)], None,
                                              ALU.mult).then_inc(pen_made, 1)
                        for m, mask in ((1, before), (2, ident)):
                            for j in range(2):
                                k = 2 * s + j
                                need(dve, pen_made, 6 * s + 2 * m + j - 1)
                                dve.scalar_tensor_tensor(prob[:, j, :], mask[:, :], cp[:, m, bass.ds(k, 1)], prob[:, j, :],
                                                         ALU.mult, ALU.add).then_inc(pen_made, 1)
                    if mlp:
                        n = HC * p + t
                        dve.wait_ge(gelu_made, n + 1)
                        if not (first and t < 2):
                            dve.wait_ge(out_done, n - 1)
                        dve.tensor_copy(h_hi[:, t % 2, :], h_slot(t)).then_inc(h_hi_made, 1)
                        dve.wait_ge(h_hi_made, n + 1)
                        dve.tensor_tensor(h_lo[:, t % 2, :], h_slot(t), h_hi[:, t % 2, :].bitcast(F32),
                                          ALU.subtract).then_inc(h_lo_made, 1)
                    if front and t == at["score"]:
                        need(dve, sc_done, s + 1)
                        need(dve, pen_made, 6 * (s + 1))
                        dve.tensor_tensor(prob[:, :, :], sc[:, 1, :].rearrange("p (j n) -> p j n", j=2), prob[:, :, :],
                                          ALU.add).then_inc(ms_made, 1)
                        need(dve, ms_made, s + 1)
                        need(dve, exp_made, 2 * s)
                        dve.tensor_reduce(nmax[:, :], prob[:, :, :], AX.X, ALU.max, negate=True).then_inc(nmax_made, 1)
                        if not mlp:
                            setup_counts()
                    for j in range(2 if front else 0):
                        k = 2 * s + j
                        if t == at["split_x"][j]:
                            split_wide_lo(xt[:, j, :], j, 3 * s)
                        if t == at["pt"][j]:
                            split_side_lo(small[:, 0, :], 4 * s + j)
                            if j == 0:
                                need(dve, exp_made, 2 * s + 2)
                                need(dve, x1_made, 2 * s)
                                dve.tensor_tensor(den[:, :], esum[:, :], cnt[:, bass.ds(2 * s, 2)], ALU.mult).then_inc(den_made, 1)
                                need(dve, den_made, s + 1)
                                dve.reciprocal(rden[:, :], den[:, :]).then_inc(rden_made, 1)
                                if not mlp:
                                    setup_stencil()
                        if t == at["pool"][j]:
                            need(dve, pool_done, k + 1)
                            need(dve, rden_made, s + 1)
                            need(dve, wide_lo_made[j], 3 * s + 1)
                            dve.scalar_tensor_tensor(xt[:, j, :], wide[:, :], rden[:, j:j + 1], xt[:, j, :],
                                                     ALU.mult, ALU.add).then_inc(x1_made, 1)
                        if t == at["down"][j]:
                            split_wide_lo(adapter(k)[1], j, 3 * s + 1)
                            split_side_lo(small[:, 1, :], 4 * s + 2 + j)
                        if t == at["up"][j]:
                            need(dve, up_done, k + 1)
                            need(dve, xb_made, 2 * k + 1)
                            dve.tensor_tensor(ya[:, j, :], wide[:, :], ya[:, j, :], ALU.add).then_inc(y_made, 1)
                            need(dve, y_made, k + 1)
                            dve.bn_stats(stats[:, :], ya[:, j, :]).then_inc(stats_made, 1)
                            need(dve, stats_made, k + 1)
                            dve.memset(vpe[:, :], EPS).then_inc(eps_set, 1)
                            dve.bn_aggr(mv[:, :], stats[:, :]).then_inc(mv_made, 1)
                            need(dve, eps_set, k + 1)
                            need(dve, mv_made, k + 1)
                            dve.tensor_tensor(vpe[:, :], mv[:, 1:2], vpe[:, :], ALU.add).then_inc(vpe_made, 1)
                        if t == at["norm"][j]:
                            need(dve, rstd_made, k + 1)
                            dve.tensor_scalar(ya[:, j, :], ya[:, j, :], mv[:, 0:1], rstd[:, 0:1], ALU.subtract,
                                              ALU.mult).then_inc(norm_made, 1)
                            need(dve, norm_made, k + 1)
                            need(dve, lng_in, 16 * (k + 1))
                            dve.tensor_tensor(ya[:, j, :], ya[:, j, :], lng_sb[:, :], ALU.mult).then_inc(scaled_made, 1)
                        if t == at["x2"][j]:
                            need(dve, scaled_made, k + 1)
                            need(dve, xb_made, 2 * k + 2)
                            need(dve, x1T_done, k + 1)
                            dve.tensor_tensor(xt[:, j, :], ya[:, j, :], x3[:, j, :], ALU.add).then_inc(x2_made, 1)
                            need(dve, x2_made, k + 1)
                            dve.tensor_scalar(ya[:, j, 0:D:D - 1], xt[:, j, 1:D - 1:D - 3], 2.0, None,
                                              ALU.mult).then_inc(edge_made, 1)
                        if t == at["lo2"][j]:
                            split_wide_lo(xt[:, j, :], j, 3 * s + 2)
                            need(dve, q_made, k + 1)
                            dve.tensor_tensor(x3[:, j, :], x3[:, j, :], xt[:, j, :], ALU.mult).then_inc(u_made, 1)
                        if t == at["lap"][j]:
                            need(dve, u_made, k + 1)
                            need(dve, edge_made, k + 1)
                            need(dve, nb_made, k + 1)
                            dve.scalar_tensor_tensor(x3[:, j, :], ya[:, j, :], zx[:, bass.ds(k, 1)], x3[:, j, :],
                                                     ALU.mult, ALU.add).then_inc(v_made, 1)
                            need(dve, v_made, k + 1)
                            need(dve, lap_done, k + 1)
                            dve.scalar_tensor_tensor(x3[:, j, :], wide[:, :], zy[:, bass.ds(k, 1)], x3[:, j, :],
                                                     ALU.mult, ALU.add).then_inc(x3_made, 1)
                    if mlp and more and t == at["split_xT"]:
                        need(dve, xT_hi_made, s)
                        dve.tensor_tensor(xT_lo, xT_v, xT_hi.bitcast(F32), ALU.subtract).then_inc(xT_lo_made, 1)
                    if front and not mlp and t in EARLY_AT:
                        split_w1_lo(EARLY_AT[t])
                    if first and t in LATE_AT:
                        split_w1_lo(LATE_AT[t])
                    if mlp and experts_at(t, SPLIT_EXPERTS):
                        ahead, c = experts_at(t, SPLIT_EXPERTS)
                        if (ahead and front) or not (ahead or first):
                            split_experts_lo(p + ahead, c)
                for j in range(2 if front else 0):
                    need(dve, x3T_hi_made, 2 * s + j + 1)
                    dve.tensor_tensor(x3T_lo[:, :, j * P:(j + 1) * P], turned[j],
                                      x3T_hi[:, :, j * P:(j + 1) * P].bitcast(F32), ALU.subtract).then_inc(x3T_lo_made, 1)

            setup()
            step(-1, True, False)
            step(0, True, True)
            with nc.vector.Fori(1, NPAIR - 2) as p:
                step(p, True, True)
            step(NPAIR - 2, True, True)
            step(NPAIR - 1, False, True)
            add_residual(NPAIR - 1)

        @block.tensor
        def _(pe):
            def mlp_in(p, t):
                n = HC * p + t
                if isinstance(p, int) and p == 0:
                    pe.wait_ge(w1_lo_made, t + 1)
                if t == 0:
                    need(pe, x3T_lo_made, 2 * (p + 1))
                need(pe, h_lo_made, n - 1)
                for c in range(DC):
                    for i, (w, v) in enumerate(((w1_hi, x3T_hi), (w1_hi, x3T_lo), (w1_lo, x3T_hi))):
                        last = pe.matmul(h_slot(t), w[:, c, t * P:(t + 1) * P], v[:, c, :], start=(c == 0 and i == 0),
                                         stop=(c == DC - 1 and i == 2))
                last.then_inc(h_done, 1)

            def mlp_out(p, t):
                n = HC * p + t
                if isinstance(p, int) and p == 0:
                    pe.wait_ge(w2_lo_made, t + 1)
                elif t % 2 == 0:
                    need(pe, e_lo_made, EPER * (p - 1) + t // 2 + 1)
                need(pe, h_lo_made, n + 1)
                if t == 0:
                    need(pe, sum_made, 4 * p)
                for j in range(2):
                    cols = slice(j * P, j * P + D)
                    for i, (v, w) in enumerate(((h_hi, w2e_hi), (h_hi, w2e_lo), (h_lo, w2e_hi))):
                        last = pe.matmul(acc[j][:, :], v[:, t % 2, j * P:(j + 1) * P], w[:, t, cols],
                                         start=(t == 0 and i == 0), stop=(t == HC - 1 and i == 2))
                last.then_inc(out_done, 1)

            def transposes(dst, src, done):
                for c in range(DC):
                    last = pe.transpose(dst[:, c, :], src[:, c * P:(c + 1) * P], ident[:, :])
                last.then_inc(done, 1)

            def split_product(dst, j, done):
                pe.matmul(dst, side_hi[:, :], wide_hi[j], start=True, stop=False)
                pe.matmul(dst, side_hi[:, :], wide_lo[j], start=False, stop=False)
                pe.matmul(dst, side_lo[:, :], wide_hi[j], start=False, stop=True).then_inc(done, 1)

            def front_piece(s, t, at, split):
                if t == at["hid"]:
                    need(pe, th_made, s)
                    if split:
                        need(pe, xT_lo_made, s - 1)
                        need(pe, l0_lo_made, 1)
                        for c in range(DC):
                            for i, (w, v) in enumerate(((l0_w1_hi, xT_hi), (l0_w1_hi, xT_lo), (l0_w1_lo, xT_hi))):
                                last = pe.matmul(sc[:, 0, :], w[:, c, :], v[:, c, :], start=(c == 0 and i == 0),
                                                 stop=(c == DC - 1 and i == 2))
                    else:
                        need(pe, xT_in, 16 * (s + 1))
                        for c in range(DC):
                            last = pe.matmul(sc[:, 0, :], l0_w1_raw[:, c, :], xT_v[:, c, :], start=(c == 0),
                                             stop=(c == DC - 1))
                    last.then_inc(hid_done, 1)
                if t == at["score"]:
                    need(pe, th_made, s + 1)
                    need(pe, ms_made, s)
                    if isinstance(s, int) and s == 0:
                        pe.wait_ge(tab, 2)
                    pe.matmul(sc[:, 1, :], vrep[:, :], th[:, :], start=True, stop=True).then_inc(sc_done, 1)
                for j in range(2):
                    k = 2 * s + j
                    if t == at["pt"][j]:
                        need(pe, exp_made, k + 1)
                        need(pe, side_lo_made, 4 * s + j)
                        pe.transpose(small[:, 0, :], prob[:, j, :], ident[:, :]).then_inc(pT_done, 1)
                    if t == at["pool"][j]:
                        need(pe, side_lo_made, 4 * s + j + 1)
                        need(pe, wide_lo_made[j], 3 * s + 1)
                        if j == 0:
                            need(pe, x3T_lo_made, 2 * s)
                        else:
                            need(pe, x1_made, k)
                        split_product(wide[:, :], j, pool_done)
                    if t == at["turn"][j]:
                        need(pe, x1_made, k + 1)
                        if j == 0:
                            need(pe, x3T_lo_made, 2 * s)
                        else:
                            need(pe, x1T_made, k)
                        transposes(turn, xt[:, j, :], x1T_done)
                    if t == at["down"][j]:
                        need(pe, x1T_made, k + 1)
                        need(pe, dw_in[j], 16 * (s + 1))
                        need(pe, side_lo_made, 4 * s + j + 2)
                        for c in range(DC):
                            last = pe.matmul(small[:, 1, :], adapter(k)[0][:, c, :], x1T_v[:, j, c, :], start=(c == 0),
                                             stop=(c == DC - 1))
                        last.then_inc(down_done, 1)
                    if t == at["up"][j]:
                        need(pe, side_lo_made, 4 * s + j + 3)
                        need(pe, wide_lo_made[j], 3 * s + 2)
                        if j == 0:
                            need(pe, x1_made, k + 2)
                        else:
                            need(pe, y_made, k)
                        split_product(wide[:, :], j, up_done)
                    if t == at["lap"][j]:
                        need(pe, wide_lo_made[j], 3 * s + 3)
                        if j == 0:
                            need(pe, y_made, k + 2)
                        else:
                            need(pe, x3_made, k)
                        pe.matmul(wide[:, :], lap[:, :], wide_hi[j], start=True, stop=False)
                        pe.matmul(wide[:, :], lap[:, :], wide_lo[j], start=False, stop=True).then_inc(lap_done, 1)

            def step(p, front, mlp):
                s = p + 1
                at = STEADY if mlp else OPENING
                for t in range(HC if mlp else OPENING_SLOTS):
                    if mlp and t == 0 and not (isinstance(p, int) and p == 0):
                        mlp_out(p - 1, HC - 1)
                    if mlp:
                        mlp_in(p, t)
                    if front:
                        front_piece(s, t, at, mlp and not (isinstance(p, int) and p == 0))
                    if front and t == (HC if mlp else OPENING_SLOTS) - 1:
                        for j in range(2):
                            need(pe, x3_made, 2 * s + j + 1)
                            if j == 0:
                                need(pe, x1T_made, 2 * s + 2)
                            transposes(turned[j], x3[:, j, :], x3T_done)
                    if mlp and t > 0:
                        mlp_out(p, t - 1)
                    if t == HC - 1 and isinstance(p, int) and p == 0:
                        pe.wait_ge(w2_lo_made, HC)

            pe.wait_ge(masks_made, MASK_OPS)
            pe.wait_ge(l0_in, 32)
            step(-1, True, False)
            step(0, True, True)
            with nc.tensor.Fori(1, NPAIR - 1) as p:
                step(p, True, True)
            step(NPAIR - 1, False, True)
            mlp_out(NPAIR - 1, HC - 1)


TAB_OPS = 19
MASK_OPS = 14


def experts_of(w2e, c):
    return w2e[:, 2 * c:2 * c + 2, :].rearrange("p h (b n) -> p h b n", n=EX)[:, :, 0:5:4, :]


def kernel(**inputs):
    import numpy as np
    import concourse.bacc as bacc
    from concourse.bass_utils import run_bass_kernel_spmd as run

    def row(name):
        return np.ascontiguousarray(inputs[name]).reshape(1, -1)

    def same(name):
        return np.ascontiguousarray(inputs[name])

    x = same("x")
    arrays = {
        "x": x,
        "xT": np.ascontiguousarray(x.reshape(NSEQ * P, D).T),
        "pt": row("itok_B_0_2"), "prof": row("itok_B_0_6"),
        "zXYR": np.concatenate([row("condB_zX"), row("condB_zY"), row("condB_zR")], axis=1),
        "expert": row("itok_B_0_7"),
        "l0_w1": same("L0_cond_W1"),
        "cols": np.ascontiguousarray(np.concatenate([same("L3_cond_b1").reshape(HC, P), row("L0_cond_b1"),
                                                     row("L0_cond_v")]).T),
        "dw": same("L1_cond_down_w"), "db": same("L1_cond_down_b"),
        "uw": same("L1_cond_up_w"), "ub": same("L1_cond_up_b"),
        "lng": same("L1_cond_ln_g"), "lnb": same("L1_cond_ln_b"),
        "w1": same("L3_cond_W1"),
        "w2": same("L3_cond_W2"), "b2": row("L3_cond_b2"),
        "we": same("L3_cond_We"), "be": same("L3_cond_be"),
    }
    nc = bacc.Bacc("TRN2", target_bir_lowering=False, num_devices=1)
    args = [nc.dram_tensor(f"in_{k}", v.shape, mybir.dt.from_np(v.dtype), kind="ExternalInput").ap()
            for k, v in arrays.items()]
    args.append(nc.dram_tensor("out_x", (NSEQ, P, D), F32, kind="ExternalOutput").ap())
    build(nc, *args)
    r = run(nc, [{f"in_{k}": v for k, v in arrays.items()}], core_ids=[0])
    return r.results[0]["out_x"]
```

```python
from contextlib import ExitStack

import concourse.bass as bass
from concourse import mybir

F32 = mybir.dt.float32
F32R = mybir.dt.float32r
I32 = mybir.dt.int32
BF16 = mybir.dt.bfloat16
ALU = mybir.AluOpType
ACT = mybir.ActivationFunctionType
AX = mybir.AxisListType

P = 128
NSEQ = 32
D = 512
DC = D // P
NPAIR = NSEQ // 2
TOK = 2 * P
HID = 2048
HC = HID // P
SH = 384
EX = 128
NEG = -1e30
EPS = 1e-5
W2C = EX + SH + EX
EPER = HC // 2
STEADY = dict(pen=0, hid=0, score=1, split_x=(3, 5), pt=(3, 5), pool=(4, 6), turn=(5, 7), down=(6, 8),
              up=(7, 9), norm=(8, 10), x2=(9, 11), hi2=(10, 12), lo2=(11, 13), lap=(12, 14), split_xT=15,
              load_bias=(5, 9), load_down=(6, 8), load_up=(6, 9), load_gain=(8, 11), load_xT=9, load_x=13)
OPENING = dict(pen=0, hid=0, score=1, split_x=(0, 1), pt=(1, 3), pool=(1, 5), turn=(4, 7), down=(6, 7),
               up=(6, 10), norm=(10, 11), x2=(11, 11), hi2=(11, 13), lo2=(13, 13), lap=(14, 15),
               load_bias=(6, 13), load_down=(10, 14), load_up=(10, 14), load_gain=(15, 19), load_xT=15,
               load_x=22)
OPENING_SLOTS = 26
RES_AT = 4
SPLIT_L0_AT = 6
LOAD_EXPERTS, SPLIT_EXPERTS = 3, 6
EARLY_LOAD = {7: 2, 12: 3, 18: 4}
EARLY_AT = {10: 0, 12: 1, 15: 2, 17: 3, 20: 4, 22: 5}
LATE_LOAD = {1: 5, 5: 6, 6: 7}
LATE_AT = {0: 6, 2: 7, 3: 8, 4: 9, 5: 10, 6: 11, 7: 12, 8: 13, 9: 14, 10: 15}


def experts_at(t, offset):
    if (t - offset) % 2:
        return None
    c = (t - offset) // 2
    return (1, c) if c >= 0 else (0, c + EPER)


def need(eng, sem, n):
    if isinstance(n, int) and n <= 0:
        return
    eng.wait_ge(sem, n)


def build(nc, x, xT, pt, prof, zXYR, expert, l0_w1, cols_src, dw, db, uw, ub, lng, lnb,
          w1, w2, b2, we, be, out):
    with ExitStack() as ctx:
        def sb(name, shape, dt=F32):
            return ctx.enter_context(nc.sbuf_tensor(name, shape, dt))

        def psum(name, shape):
            return ctx.enter_context(nc.psum_tensor(name, shape, F32))

        def sem(name):
            return ctx.enter_context(nc.semaphore(name))

        shapes = dict(w1=[P, DC, HID], w2e=[P, HC, W2C], l0_w1=[P, DC, P], xT=[P, DC * TOK])
        with ExitStack() as loaded:
            w1_raw, w2e_raw, l0_w1_raw, xT_raw = (loaded.enter_context(nc.sbuf_tensor(f"{n}_raw", shape, F32))
                                                  for n, shape in shapes.items())
        w1_lo, w2e_lo, l0_w1_lo, xT_lo = (sb(f"{n}_lo", shape, F32R) for n, shape in shapes.items())
        w1_hi, w2e_hi, l0_w1_hi = (sb(f"{n}_hi", shapes[n], F32R) for n in ("w1", "w2e", "l0_w1"))
        res = sb("res", [P, 2, D])
        x3T_hi = sb("x3T_hi", [P, DC, TOK], F32R)
        x3T_lo = sb("x3T_lo", [P, DC, TOK], F32R)
        h_hi = sb("h_hi", [P, 2, TOK], F32R)
        h_lo = sb("h_lo", [P, 2, TOK], F32R)
        x3 = sb("x3", [P, 2, D])
        xT_v = xT_raw[:, :].rearrange("p (c n) -> p c n", c=DC)
        x1T_v = xT_raw[:, :].rearrange("p (j c n) -> p j c n", j=2, c=DC)
        xT_lo = xT_lo[:, :].rearrange("p (c n) -> p c n", c=DC)
        xt = sb("xt", [P, 2, D])
        ya = sb("ya", [P, 2, D])
        scratch = [sb("scratch0", [P, 2 * D], F32R), sb("scratch1", [P, 2 * D], F32R)]
        wide_hi, wide_lo = [a[:, 0:D] for a in scratch], [a[:, D:2 * D] for a in scratch]
        xT_hi = scratch[0][:, :].rearrange("p (c n) -> p c n", c=DC)
        side_hi = sb("side_hi", [P, P], F32R)
        side_lo = sb("side_lo", [P, P], F32R)
        dw_sb = sb("dw_sb", [P, DC, P])
        uw_sb = sb("uw_sb", [P, D])

        def adapter(k):
            if isinstance(k, int) and k == 1:
                return res[:, 0, :].rearrange("p (c n) -> p c n", c=DC), res[:, 1, :]
            return dw_sb[:, :, :], uw_sb[:, :]

        db_sb = sb("db_sb", [P, 2])
        ub_sb = sb("ub_sb", [P, D])
        lng_sb = sb("lng_sb", [P, D])
        lnb_sb = sb("lnb_sb", [P, D])

        def tables(k):
            if isinstance(k, int) and k == 1:
                return [w2e_raw[:, HC - 3 + i, 0:D] for i in range(3)]
            return [ub_sb[:, :], lnb_sb[:, :], lng_sb[:, :]]

        be_sb = sb("be_sb", [P, 2, EX])
        b2_sb = sb("b2_sb", [P, SH])
        th = sb("th", [P, TOK])
        prob = sb("prob", [P, 2, P])
        vrep = sb("vrep", [P, P])
        ident = sb("ident", [P, P])
        after = sb("after", [P, P], BF16)
        before = sb("before", [P, P], BF16)
        lap = sb("lap", [P, P], F32R)
        cols = sb("cols", [P, HC + 2])
        b1_sb, l0_b1_sb, l0_v_sb = cols[:, 0:HC], cols[:, HC:HC + 1], cols[:, HC + 1:HC + 2]
        idx = sb("idx", [1, 2, NSEQ], I32)
        pt_i = sb("pt_i", [P, NSEQ], I32)
        zxyr = sb("zxyr", [P, 3, NSEQ])
        zx, zy, zr = (zxyr[:, i, :] for i in range(3))
        nzr = sb("nzr", [P, NSEQ])
        qb = sb("qb", [P, NSEQ])
        cp = sb("cp", [P, 3, NSEQ])
        cnt = sb("cnt", [P, NSEQ])
        rows = sb("rows", [P, 2])
        half = sb("half", [P, 1])
        nmax = sb("nmax", [P, 2])
        esum = sb("esum", [P, 2])
        den = sb("den", [P, 2])
        rden = sb("rden", [P, 2])
        stats = sb("stats", [P, 2, 6])
        mv = sb("mv", [P, 2, 2])
        vpe = sb("vpe", [P, 2])
        warm = sb("warm", [P, 1])
        rstd = sb("rstd", [P, 2])

        acc = [psum("acc0", [P, D]), psum("acc1", [P, D])]
        h_ps = [psum("h_ps0", [P, D]), psum("h_ps1", [P, D])]
        sc = psum("sc", [P, 2, TOK])
        small = psum("small", [P, 4, P])
        turn = psum("turn", [P, DC, P])
        wide = psum("wide", [P, D])
        turned = [turn[:, :, :], wide[:, :].rearrange("p (c n) -> p c n", c=DC)]

        def wide_of(j, mlp):
            return wide[:, :] if mlp or j == 0 else acc[1][:, :]

        def h_slot(t):
            return h_ps[t % 2][:, 0:TOK]


        hid_in = [sem("hid_in0"), sem("hid_in1")]
        cols_in, pt_in, z_in, b2_in, idx_in = (sem(n) for n in ("cols_in", "pt_in", "z_in", "b2_in", "idx_in"))
        masks_made = sem("masks_made")
        tab = sem("tab")
        w_in = [sem(f"w_in{g}") for g in range(HC // 2)]
        w1_hi_made, w1_lo_made = sem("w1_hi_made"), sem("w1_lo_made")
        w2_hi_made, w2_lo_made = sem("w2_hi_made"), sem("w2_lo_made")
        e_hi_made, e_lo_made = sem("e_hi_made"), sem("e_lo_made")
        xT_in, x_in = sem("xT_in"), sem("x_in")
        dw_in, uw_in = [sem("dw_in0"), sem("dw_in1")], [sem("uw_in0"), sem("uw_in1")]
        ub_in, lnb_in, lng_in = ([sem(f"{n}0"), sem(f"{n}1")] for n in ("ub_in", "lnb_in", "lng_in"))
        be_in = sem("be_in")
        hid_done, th_made, sc_done = sem("hid_done"), sem("th_made"), sem("sc_done")
        pen_made, ms_made, nmax_made = sem("pen_made"), sem("ms_made"), sem("nmax_made")
        exp_made, den_made, rden_made = sem("exp_made"), sem("den_made"), sem("rden_made")
        pT_done, pool_done, x1_made = sem("pT_done"), sem("pool_done"), sem("x1_made")
        wide_hi_made = [sem("wide_hi_made0"), sem("wide_hi_made1")]
        wide_lo_made = [sem("wide_lo_made0"), sem("wide_lo_made1")]
        side_hi_made, side_lo_made = sem("side_hi_made"), sem("side_lo_made")
        xb_made = sem("xb_made")
        x1T_done, x1T_made = sem("x1T_done"), sem("x1T_made")
        xT_hi_made, xT_lo_made = sem("xT_hi_made"), sem("xT_lo_made")
        l0_hi_made, l0_lo_made = sem("l0_hi_made"), sem("l0_lo_made")
        down_done, z_made, up_done = sem("down_done"), sem("z_made"), sem("up_done")
        y_made, stats_made, mv_made = sem("y_made"), sem("stats_made"), sem("mv_made")
        eps_set, vpe_made, rstd_made = sem("eps_set"), sem("vpe_made"), sem("rstd_made")
        norm_made, scaled_made = sem("norm_made"), sem("scaled_made")
        x2_made, edge_made = sem("x2_made"), sem("edge_made")
        nb_made, q_made, u_made = sem("nb_made"), sem("q_made"), sem("u_made")
        v_made, lap_done, x3_made = sem("v_made"), sem("lap_done"), sem("x3_made")
        x3T_done, x3T_hi_made, x3T_lo_made = sem("x3T_done"), sem("x3T_hi_made"), sem("x3T_lo_made")
        h_done, gelu_made = sem("h_done"), sem("gelu_made")
        h_hi_made, h_lo_made = sem("h_hi_made"), sem("h_lo_made")
        out_done = sem("out_done")
        acc0_done = sem("acc0_done")
        res_made, sum_made, stored = sem("res_made"), sem("sum_made"), sem("stored")

        block = ctx.enter_context(nc.Block())

        @block.sync
        def _(sp):
            def index(row, k):
                return nc.sync.value_load(idx[0:1, row, bass.ds(k, 1)], min_val=0, max_val=7)

            def load_xT(s):
                need(sp, down_done, 2 * s)
                sp.dma_start(xT_v, xT[:, bass.ds(s * TOK, TOK)].rearrange("(c p) n -> p c n", p=P)).then_inc(xT_in, 16)

            def load_x(s):
                for j in range(2):
                    need(sp, wide_lo_made[j], 3 * s)
                need(sp, u_made, 2 * s)
                need(sp, nb_made, 2 * s)
                sp.dma_start(xt[:, :, :], x[bass.ds(2 * s, 2)].rearrange("j p n -> p j n")).then_inc(x_in, 16)

            def load_down(e, j, k):
                need(sp, z_made, 0 if isinstance(k, int) and k == 1 else k)
                sp.dma_start(adapter(k)[0], dw[bass.ds(e, 1)].rearrange("a (c p) n -> p (a c) n", p=P)).then_inc(dw_in[j], 16)
                sp.dma_start(db_sb[:, j:j + 1], db[bass.ds(e, 1)].rearrange("a (p o) -> p (a o)", o=1)).then_inc(dw_in[j], 16)

            def load_up_weights(e, j, k):
                sp.dma_start(adapter(k)[1], uw[bass.ds(e, 1)].rearrange("a p n -> p (a n)")).then_inc(uw_in[j], 16)

            def load_up(e, j, split_before):
                need(sp, wide_lo_made[1 - j], split_before)
                load_up_weights(e, j, None)

            def every(src, e):
                return src[bass.ds(e, 1)].rearrange("a n -> (a n)").partition_broadcast(P)

            def load_biases(e, j, k):
                up_bias, norm_bias, _ = tables(k)
                need(sp, xb_made, 0 if isinstance(k, int) and k == 1 else 2 * k)
                sp.dma_start(up_bias, every(ub, e)).then_inc(ub_in[j], 16)
                sp.dma_start(norm_bias, every(lnb, e)).then_inc(lnb_in[j], 16)

            def load_gain(e, j, k):
                need(sp, scaled_made, 0 if isinstance(k, int) and k == 1 else k)
                sp.dma_start(tables(k)[2], every(lng, e)).then_inc(lng_in[j], 16)

            def load_expert_bias(es, p):
                need(sp, res_made, 4 * p)
                for j in range(2):
                    sp.dma_start(be_sb[:, j, :], every(be, es[j])).then_inc(be_in, 16)

            def load_weights(g, es):
                if g >= HC // 2 - 2:
                    sp.wait_ge(xb_made, 4)
                    sp.wait_ge(scaled_made, 2)
                two, rows_ = slice(2 * g, 2 * g + 2), slice(2 * g * P, 2 * (g + 1) * P)
                sp.dma_start(w1_raw[:, :, rows_], w1[:, rows_].rearrange("(c p) n -> p c n", p=P)).then_inc(w_in[g], 16)
                sp.dma_start(w2e_raw[:, two, EX:EX + SH],
                             w2[rows_, :].rearrange("(h p) n -> p h n", p=P)).then_inc(w_in[g], 16)
                for j in range(2):
                    load_expert(g, j, es[j], w_in[g])

            def load_expert(c, j, e, landed):
                at = j * (EX + SH)
                sp.dma_start(w2e_raw[:, 2 * c:2 * c + 2, at:at + EX],
                             we[bass.ds(e, 1), 2 * c * P:2 * (c + 1) * P, :].rearrange(
                                 "a (h p) n -> p (a h) n", p=P)).then_inc(landed, 16)

            def load_experts(p, c, es):
                sp.wait_ge(out_done, HC * (p - 1) + 2 * c + 2)
                for j in range(2):
                    load_expert(c, j, es[j], w_in[c])

            def store(p):
                for j in range(2):
                    sp.wait_ge(sum_made, 4 * p + 2 * j + 2)
                    sp.dma_start(out[bass.ds(2 * p + j, 1)].rearrange("a p n -> p (a n)"), res[:, j, :]).then_inc(stored, 16)

            def step(p, front, mlp):
                s = p + 1
                at = STEADY if mlp else OPENING
                more = front and not (isinstance(s, int) and s == NPAIR - 1)
                if mlp:
                    es = [index(1, 2 * p + j) for j in range(2)]
                if mlp and front:
                    es_next = [index(1, 2 * s + j) for j in range(2)]
                if front:
                    e1 = index(0, 2 * s + 1)
                if more:
                    e2 = index(0, 2 * s + 2)
                first = isinstance(p, int) and p == 0
                for t in range(HC if mlp else OPENING_SLOTS):
                    if mlp and t == 1 and not first:
                        store(p - 1)
                    if mlp and experts_at(t, LOAD_EXPERTS):
                        ahead, c = experts_at(t, LOAD_EXPERTS)
                        if (ahead and front) or not (ahead or first):
                            load_experts(p + ahead, c, es_next if ahead else es)
                    if mlp and front and t == 4:
                        load_expert_bias(es_next, s)
                    if front and mlp and t == at["load_bias"][0]:
                        load_biases(e1, 1, 2 * s + 1)
                    if front and mlp and t == at["load_down"][0]:
                        load_down(e1, 1, 2 * s + 1)
                    if front and mlp and t == at["load_up"][0]:
                        load_up(e1, 1, 3 * s + 2)
                    if front and mlp and t == at["load_gain"][0]:
                        load_gain(e1, 1, 2 * s + 1)
                    if more and t == at["load_xT"]:
                        load_xT(s + 1)
                    if more and t == at["load_down"][1]:
                        load_down(e2, 0, 2 * s + 2)
                    if more and t == at["load_up"][1]:
                        load_up(e2, 0, 3 * s + 2)
                    if more and t == at["load_bias"][1]:
                        load_biases(e2, 0, 2 * s + 2)
                    if more and t == at["load_gain"][1]:
                        load_gain(e2, 0, 2 * s + 2)
                    if more and t == at["load_x"]:
                        load_x(s + 1)
                    if front and not mlp and t in EARLY_LOAD:
                        load_weights(EARLY_LOAD[t], es_first)
                    if first and t in LATE_LOAD:
                        load_weights(LATE_LOAD[t], es)

            for h in range(2):
                half_c, half_rows = slice(h * DC // 2, (h + 1) * DC // 2), slice(h * D // 2, (h + 1) * D // 2)
                sp.dma_start(l0_w1_raw[:, half_c, :], l0_w1[half_rows, :].rearrange("(c p) n -> p c n", p=P)).then_inc(hid_in[h], 16)
                sp.dma_start(xT_v[:, half_c, :], xT[half_rows, 0:TOK].rearrange("(c p) n -> p c n", p=P)).then_inc(hid_in[h], 16)
            sp.dma_start(cols[:, :], cols_src).then_inc(cols_in, 16)
            sp.dma_start(pt_i[:, :], pt.rearrange("a n -> (a n)").partition_broadcast(P)).then_inc(pt_in, 16)
            sp.dma_start(idx[:, 0, :], prof).then_inc(idx_in, 16)
            sp.dma_start(idx[:, 1, :], expert).then_inc(idx_in, 16)
            load_x(0)
            sp.dma_start(zxyr[:, :, :].rearrange("p a n -> p (a n)"),
                         zXYR.rearrange("a n -> (a n)").partition_broadcast(P)).then_inc(z_in, 16)
            sp.wait_ge(idx_in, 32)
            e_first = index(0, 0)
            es_first = [index(1, j) for j in range(2)]
            load_biases(e_first, 0, 0)
            load_down(e_first, 0, 0)
            load_up(e_first, 0, 0)
            e_second = index(0, 1)
            load_weights(0, es_first)
            load_down(e_second, 1, 1)
            load_up_weights(e_second, 1, 1)
            load_gain(e_first, 0, 0)
            load_biases(e_second, 1, 1)
            load_gain(e_second, 1, 1)
            load_weights(1, es_first)
            sp.dma_start(b2_sb[:, :], b2.rearrange("a n -> (a n)").partition_broadcast(P)).then_inc(b2_in, 16)
            load_expert_bias(es_first, 0)
            step(-1, True, False)
            step(0, True, True)
            with nc.sync.Fori(1, NPAIR - 2) as p:
                step(p, True, True)
            step(NPAIR - 2, True, True)
            step(NPAIR - 1, False, True)
            store(NPAIR - 1)
            sp.wait_ge(stored, 32 * NPAIR)

        @block.gpsimd
        def _(pool):
            def fill(tile, value):
                pool.memset(tile, value).then_inc(masks_made, 1)

            fill(ident[:, :], 0.0)
            fill(after[:, :], 0.0)
            fill(before[:, :], 0.0)
            lap_raw = ya[:, 0, 0:P]
            fill(lap_raw, 0.0)
            fill(half[:, :], -0.5)
            pool.wait_ge(masks_made, 5)

            def mark(tile, value, base, step_p, step_f, op, n=P):
                pool.affine_select(out=tile, in_=tile, compare_op=op, fill=value, base=base,
                                   pattern=[[step_f, n]], channel_multiplier=step_p).then_inc(masks_made, 1)

            mark(ident[:, :], 1.0, 0, 1, -1, ALU.not_equal)
            mark(after[:, :], 1.0, 0, 1, -1, ALU.is_ge)
            mark(before[:, :], 1.0, 0, -1, 1, ALU.is_ge)
            mark(lap_raw, -2.0, 0, 1, -1, ALU.not_equal)
            pool.wait_ge(masks_made, 9)
            mark(lap_raw, 1.0, -1, 1, -1, ALU.not_equal)
            pool.wait_ge(masks_made, 10)
            mark(lap_raw, 1.0, 1, 1, -1, ALU.not_equal)
            pool.wait_ge(masks_made, 11)
            mark(lap_raw[:, 0:1], 2.0, -1, 1, 0, ALU.not_equal, 1)
            mark(lap_raw[:, P - 1:P], 2.0, -(P - 2), 1, 0, ALU.not_equal, 1)
            pool.wait_ge(masks_made, 13)
            pool.tensor_copy(lap[:, :], lap_raw).then_inc(masks_made, 1)

            def split_w2_lo(w):
                pool.wait_ge(w2_hi_made, w + 1)
                pool.tensor_tensor(w2e_lo[:, w, :], w2e_raw[:, w, :], w2e_hi[:, w, :].bitcast(F32),
                                   ALU.subtract).then_inc(w2_lo_made, 1)

            def step(p, front, mlp):
                s = p + 1
                at = STEADY if mlp else OPENING
                first = isinstance(p, int) and p == 0
                for t in range(HC if mlp else OPENING_SLOTS):
                    if mlp and t == RES_AT:
                        need(pool, stored, 32 * p)
                        need(pool, x3_made, 2 * (p + 1))
                        need(pool, be_in, 32 * (p + 1))
                        if isinstance(p, int) and p == 0:
                            pool.wait_ge(b2_in, 16)
                        for j in range(2):
                            pool.tensor_tensor(res[:, j, 0:SH], x3[:, j, 0:SH], b2_sb[:, :], ALU.add).then_inc(res_made, 1)
                            pool.tensor_tensor(res[:, j, SH:D], x3[:, j, SH:D], be_sb[:, j, :], ALU.add).then_inc(res_made, 1)
                    for j in range(2 if front else 0):
                        k = 2 * s + j
                        if t == at["pool"][j]:
                            need(pool, x1_made, k + 1)
                            need(pool, v_made, k - 1)
                            need(pool, ub_in[j], 16 * (s + 1))
                            pool.tensor_tensor(ya[:, j, :], xt[:, j, :], tables(k)[0], ALU.add).then_inc(xb_made, 1)
                            need(pool, lnb_in[j], 16 * (s + 1))
                            need(pool, x3T_done, 2 * s)
                            need(pool, res_made, 4 * s)
                            pool.tensor_tensor(x3[:, j, :], xt[:, j, :], tables(k)[1], ALU.add).then_inc(xb_made, 1)
                        if t == at["up"][j]:
                            need(pool, vpe_made, k + 1)
                            pool.tensor_tensor(rstd[:, j:j + 1], vpe[:, j:j + 1], half[:, :], ALU.pow).then_inc(rstd_made, 1)
                        if t == at["x2"][j]:
                            need(pool, x2_made, k + 1)
                            pool.tensor_tensor(ya[:, j, 1:D - 1], xt[:, j, 0:D - 2], xt[:, j, 2:D], ALU.add).then_inc(nb_made, 1)
                    if front and not mlp and t in EARLY_AT:
                        split_w2_lo(EARLY_AT[t])
                    if first and t in LATE_AT:
                        split_w2_lo(LATE_AT[t])

            step(-1, True, False)
            step(0, True, True)
            with nc.gpsimd.Fori(1, NPAIR - 1) as p:
                step(p, True, True)
            step(NPAIR - 1, False, True)

        @block.scalar
        def _(act):
            def split_weights_hi(w):
                act.wait_ge(w_in[w // 2], 64)
                act.copy(w1_hi[:, :, w * P:(w + 1) * P], w1_raw[:, :, w * P:(w + 1) * P]).then_inc(w1_hi_made, 1)
                act.copy(w2e_hi[:, w, :], w2e_raw[:, w, :]).then_inc(w2_hi_made, 1)

            def split_experts_hi(p, c):
                act.wait_ge(w_in[c], 64 + 32 * p)
                act.copy(experts_of(w2e_hi, c), experts_of(w2e_raw, c)).then_inc(e_hi_made, 1)

            def step(p, front, mlp):
                s = p + 1
                at = STEADY if mlp else OPENING
                more = front and not (isinstance(s, int) and s == NPAIR - 1)
                first = isinstance(p, int) and p == 0
                for t in range(HC if mlp else OPENING_SLOTS):
                    if mlp:
                        n = HC * p + t
                        act.wait_ge(h_done, n + 1)
                        act.activation(h_slot(t), h_slot(t), ACT.Gelu, bias=b1_sb[:, t:t + 1]).then_inc(gelu_made, 1)
                    if first and t == SPLIT_L0_AT:
                        act.copy(l0_w1_hi[:, :, :], l0_w1_raw[:, :, :]).then_inc(l0_hi_made, 1)
                    if front and t == at["hid"]:
                        need(act, hid_done, s + 1)
                        need(act, sc_done, s)
                        act.activation(th[:, :], sc[:, 0, :], ACT.Tanh, bias=l0_b1_sb[:, 0:1]).then_inc(th_made, 1)
                    if front and t == at["score"]:
                        need(act, nmax_made, s + 1)
                        for j in range(2):
                            act.activation(prob[:, j, :], prob[:, j, :], ACT.Exp, bias=nmax[:, j:j + 1],
                                           accum_out=esum[:, j:j + 1]).then_inc(exp_made, 1)
                    for j in range(2 if front else 0):
                        k = 2 * s + j
                        if t == at["split_x"][j]:
                            need(act, x_in, 16 * (s + 1))
                            need(act, lap_done, k - 1)
                            act.copy(wide_hi[j], xt[:, j, :]).then_inc(wide_hi_made[j], 1)
                        if t == at["pt"][j]:
                            if j == 0:
                                need(act, up_done, k)
                            else:
                                need(act, pool_done, k)
                            need(act, pT_done, k + 1)
                            act.copy(side_hi[:, :], small[:, 0, :]).then_inc(side_hi_made, 1)
                        if t == at["turn"][j]:
                            need(act, x1T_done, k + 1)
                            act.copy(x1T_v[:, j, :, :], turn[:, :, :]).then_inc(x1T_made, 1)
                        if t == at["down"][j]:
                            need(act, uw_in[j], 16 * (s + 1))
                            need(act, pool_done, k + 1)
                            act.copy(wide_hi[j], adapter(k)[1]).then_inc(wide_hi_made[j], 1)
                            need(act, down_done, k + 1)
                            need(act, dw_in[j], 32 * (s + 1))
                            act.activation(small[:, 1, :], small[:, 1, :], ACT.Relu, bias=db_sb[:, j:j + 1]).then_inc(z_made, 1)
                            need(act, z_made, k + 1)
                            if j == 0:
                                need(act, pool_done, k + 2)
                            else:
                                need(act, up_done, k)
                            act.copy(side_hi[:, :], small[:, 1, :]).then_inc(side_hi_made, 1)
                        if t == at["hi2"][j]:
                            need(act, x2_made, k + 1)
                            need(act, up_done, k + 1)
                            act.copy(wide_hi[j], xt[:, j, :]).then_inc(wide_hi_made[j], 1)
                            if isinstance(k, int) and k == 0:
                                act.wait_ge(tab, TAB_OPS)
                            act.activation(x3[:, j, :], xt[:, j, :], ACT.Identity, bias=qb[:, bass.ds(k, 1)],
                                           scale=nzr[:, bass.ds(k, 1)]).then_inc(q_made, 1)
                    if mlp and more and t == at["split_xT"]:
                        need(act, lap_done, 2 * s + 1)
                        need(act, xT_in, 16 * (s + 1))
                        act.copy(xT_hi, xT_v).then_inc(xT_hi_made, 1)
                    if front and not mlp and t in EARLY_AT:
                        split_weights_hi(EARLY_AT[t])
                    if first and t in LATE_AT:
                        split_weights_hi(LATE_AT[t])
                    if mlp and experts_at(t, SPLIT_EXPERTS):
                        ahead, c = experts_at(t, SPLIT_EXPERTS)
                        if (ahead and front) or not (ahead or first):
                            split_experts_hi(p + ahead, c)
                for j in range(2 if front else 0):
                    need(act, x3T_done, 2 * s + j + 1)
                    act.copy(x3T_hi[:, :, j * P:(j + 1) * P], turned[j]).then_inc(x3T_hi_made, 1)

            act.wait_ge(masks_made, 5)
            act.activation(warm[:, :], half[:, :], ACT.Tanh)
            act.wait_ge(cols_in, 16)
            step(-1, True, False)
            step(0, True, True)
            with nc.scalar.Fori(1, NPAIR - 2) as p:
                step(p, True, True)
            step(NPAIR - 2, True, True)
            step(NPAIR - 1, False, True)

        @block.vector
        def _(dve):
            made = [0]

            def table(ins):
                made[0] += 1
                ins.then_inc(tab, 1)
                dve.wait_ge(tab, made[0])

            def setup():
                table(dve.memset(vrep[:, :], 1.0))
                dve.wait_ge(masks_made, 8)
                table(dve.tensor_reduce(rows[:, 0:1], after[:, :], AX.X, ALU.add))
                table(dve.tensor_reduce(rows[:, 1:2], before[:, :], AX.X, ALU.add))
                table(dve.tensor_scalar(rows[:, :], rows[:, :], -1.0, float(P), ALU.mult, ALU.add))
                dve.wait_ge(cols_in, 16)
                table(dve.tensor_scalar(vrep[:, :], vrep[:, :], l0_v_sb[:, 0:1], None, ALU.mult))
                dve.wait_ge(pt_in, 16)
                table(dve.tensor_copy(cnt[:, :], pt_i[:, :]))
                table(dve.tensor_scalar(cp[:, 0, :], cnt[:, :], 0.0, NEG, ALU.is_equal, ALU.mult))
                table(dve.tensor_scalar(cp[:, 1, :], cnt[:, :], 1.0, NEG, ALU.is_equal, ALU.mult))
                table(dve.tensor_tensor(cp[:, 2, :], cp[:, 0, :], cp[:, 1, :], ALU.add))
                table(dve.tensor_scalar(cp[:, 2, :], cp[:, 2, :], -1.0, NEG, ALU.mult, ALU.add))

            def setup_counts():
                table(dve.tensor_scalar(nzr[:, :], cnt[:, :], 0.0, None, ALU.is_equal))
                table(dve.tensor_scalar(qb[:, :], cnt[:, :], 1.0, None, ALU.is_equal))
                table(dve.tensor_tensor(cnt[:, :], nzr[:, :], qb[:, :], ALU.add))
                table(dve.tensor_scalar(cnt[:, :], cnt[:, :], -float(P - 1), float(P - 1), ALU.mult, ALU.add))
                table(dve.scalar_tensor_tensor(cnt[:, :], nzr[:, :], rows[:, 0:1], cnt[:, :], ALU.mult, ALU.add))
                table(dve.scalar_tensor_tensor(cnt[:, :], qb[:, :], rows[:, 1:2], cnt[:, :], ALU.mult, ALU.add))

            def setup_stencil():
                dve.wait_ge(z_in, 16)
                table(dve.tensor_scalar(nzr[:, :], zr, -1.0, None, ALU.mult))
                table(dve.tensor_scalar(qb[:, :], zr, 1.0, None, ALU.add))
                table(dve.scalar_tensor_tensor(qb[:, :], zx, -2.0, qb[:, :], ALU.mult, ALU.add))

            def split_w1_lo(w):
                part = slice(w * P, (w + 1) * P)
                dve.wait_ge(w1_hi_made, w + 1)
                dve.tensor_tensor(w1_lo[:, :, part], w1_raw[:, :, part], w1_hi[:, :, part].bitcast(F32),
                                  ALU.subtract).then_inc(w1_lo_made, 1)

            def split_wide_lo(source, j, w):
                need(dve, wide_hi_made[j], w + 1)
                dve.tensor_tensor(wide_lo[j], source, wide_hi[j].bitcast(F32), ALU.subtract).then_inc(wide_lo_made[j], 1)

            def split_side_lo(source, v):
                need(dve, side_hi_made, v + 1)
                dve.tensor_tensor(side_lo[:, :], source, side_hi[:, :].bitcast(F32), ALU.subtract).then_inc(side_lo_made, 1)

            def split_experts_lo(p, c):
                dve.wait_ge(e_hi_made, EPER * (p - 1) + c + 1)
                dve.tensor_tensor(experts_of(w2e_lo, c), experts_of(w2e_raw, c),
                                  experts_of(w2e_hi, c).bitcast(F32), ALU.subtract).then_inc(e_lo_made, 1)

            def add_residual(p):
                final = isinstance(p, int) and p == NPAIR - 1
                if final:
                    dve.wait_ge(acc0_done, 1)
                else:
                    dve.wait_ge(out_done, HC * (p + 1))
                need(dve, res_made, 4 * (p + 1))
                for j, cols, at in ((0, slice(0, SH), EX), (0, slice(SH, D), 0), (1, slice(0, SH), 0), (1, slice(SH, D), SH)):
                    if final and j == 1 and at == 0:
                        dve.wait_ge(out_done, HC * (p + 1))
                    dve.tensor_tensor(res[:, j, cols], acc[j][:, at:at + cols.stop - cols.start], res[:, j, cols],
                                      ALU.add).then_inc(sum_made, 1)

            def step(p, front, mlp):
                s = p + 1
                at = STEADY if mlp else OPENING
                more = front and not (isinstance(s, int) and s == NPAIR - 1)
                first = isinstance(p, int) and p == 0
                for t in range(HC if mlp else OPENING_SLOTS):
                    if mlp and t == 0 and not first:
                        add_residual(p - 1)
                    if first and t == SPLIT_L0_AT:
                        dve.wait_ge(l0_hi_made, 1)
                        dve.wait_ge(hid_done, 2)
                        dve.tensor_tensor(l0_w1_lo[:, :, :], l0_w1_raw[:, :, :], l0_w1_hi[:, :, :].bitcast(F32),
                                          ALU.subtract).then_inc(l0_lo_made, 1)
                    if front and t == at["pen"]:
                        need(dve, pT_done, 2 * s)
                        for j in range(2):
                            k = 2 * s + j
                            dve.tensor_scalar(prob[:, j, :], after[:, :], cp[:, 0, bass.ds(k, 1)], None,
                                              ALU.mult).then_inc(pen_made, 1)
                        for m, mask in ((1, before), (2, ident)):
                            for j in range(2):
                                k = 2 * s + j
                                need(dve, pen_made, 6 * s + 2 * m + j - 1)
                                dve.scalar_tensor_tensor(prob[:, j, :], mask[:, :], cp[:, m, bass.ds(k, 1)], prob[:, j, :],
                                                         ALU.mult, ALU.add).then_inc(pen_made, 1)
                    if mlp:
                        n = HC * p + t
                        dve.wait_ge(gelu_made, n + 1)
                        if not (first and t < 2):
                            dve.wait_ge(out_done, n - 1)
                        dve.tensor_copy(h_hi[:, t % 2, :], h_slot(t)).then_inc(h_hi_made, 1)
                        dve.wait_ge(h_hi_made, n + 1)
                        dve.tensor_tensor(h_lo[:, t % 2, :], h_slot(t), h_hi[:, t % 2, :].bitcast(F32),
                                          ALU.subtract).then_inc(h_lo_made, 1)
                    if front and t == at["score"]:
                        need(dve, sc_done, s + 1)
                        need(dve, pen_made, 6 * (s + 1))
                        dve.tensor_tensor(prob[:, :, :], sc[:, 1, :].rearrange("p (j n) -> p j n", j=2), prob[:, :, :],
                                          ALU.add).then_inc(ms_made, 1)
                        need(dve, ms_made, s + 1)
                        need(dve, exp_made, 2 * s)
                        dve.tensor_reduce(nmax[:, :], prob[:, :, :], AX.X, ALU.max, negate=True).then_inc(nmax_made, 1)
                        if not mlp:
                            setup_counts()
                    for j in range(2 if front else 0):
                        k = 2 * s + j
                        if t == at["split_x"][j]:
                            split_wide_lo(xt[:, j, :], j, 3 * s)
                        if t == at["pt"][j]:
                            split_side_lo(small[:, 0, :], 4 * s + j)
                            if j == 0:
                                need(dve, exp_made, 2 * s + 2)
                                need(dve, x1_made, 2 * s)
                                dve.tensor_tensor(den[:, :], esum[:, :], cnt[:, bass.ds(2 * s, 2)], ALU.mult).then_inc(den_made, 1)
                                need(dve, den_made, s + 1)
                                dve.reciprocal(rden[:, :], den[:, :]).then_inc(rden_made, 1)
                                if not mlp:
                                    setup_stencil()
                        if t == at["pool"][j]:
                            need(dve, pool_done, k + 1)
                            need(dve, rden_made, s + 1)
                            need(dve, wide_lo_made[j], 3 * s + 1)
                            dve.scalar_tensor_tensor(xt[:, j, :], wide_of(j, mlp), rden[:, j:j + 1], xt[:, j, :],
                                                     ALU.mult, ALU.add).then_inc(x1_made, 1)
                        if t == at["down"][j]:
                            split_wide_lo(adapter(k)[1], j, 3 * s + 1)
                            split_side_lo(small[:, 1, :], 4 * s + 2 + j)
                        if t == at["up"][j]:
                            need(dve, up_done, k + 1)
                            need(dve, xb_made, 2 * k + 1)
                            dve.tensor_tensor(ya[:, j, :], wide_of(j, mlp), ya[:, j, :], ALU.add).then_inc(y_made, 1)
                            need(dve, y_made, k + 1)
                            dve.bn_stats(stats[:, j, :], ya[:, j, :]).then_inc(stats_made, 1)
                            need(dve, stats_made, k + 1)
                            dve.memset(vpe[:, j:j + 1], EPS).then_inc(eps_set, 1)
                            dve.bn_aggr(mv[:, j, :], stats[:, j, :]).then_inc(mv_made, 1)
                            need(dve, eps_set, k + 1)
                            need(dve, mv_made, k + 1)
                            dve.tensor_tensor(vpe[:, j:j + 1], mv[:, j, 1:2], vpe[:, j:j + 1], ALU.add).then_inc(vpe_made, 1)
                        if t == at["norm"][j]:
                            need(dve, rstd_made, k + 1)
                            dve.tensor_scalar(ya[:, j, :], ya[:, j, :], mv[:, j, 0:1], rstd[:, j:j + 1], ALU.subtract,
                                              ALU.mult).then_inc(norm_made, 1)
                            need(dve, norm_made, k + 1)
                            need(dve, lng_in[j], 16 * (s + 1))
                            dve.tensor_tensor(ya[:, j, :], ya[:, j, :], tables(k)[2], ALU.mult).then_inc(scaled_made, 1)
                        if t == at["x2"][j]:
                            need(dve, scaled_made, k + 1)
                            need(dve, xb_made, 2 * k + 2)
                            need(dve, x1T_done, k + 1)
                            dve.tensor_tensor(xt[:, j, :], ya[:, j, :], x3[:, j, :], ALU.add).then_inc(x2_made, 1)
                            need(dve, x2_made, k + 1)
                            dve.tensor_scalar(ya[:, j, 0:D:D - 1], xt[:, j, 1:D - 1:D - 3], 2.0, None,
                                              ALU.mult).then_inc(edge_made, 1)
                        if t == at["lo2"][j]:
                            split_wide_lo(xt[:, j, :], j, 3 * s + 2)
                            need(dve, q_made, k + 1)
                            dve.tensor_tensor(x3[:, j, :], x3[:, j, :], xt[:, j, :], ALU.mult).then_inc(u_made, 1)
                        if t == at["lap"][j]:
                            need(dve, u_made, k + 1)
                            need(dve, edge_made, k + 1)
                            need(dve, nb_made, k + 1)
                            dve.scalar_tensor_tensor(x3[:, j, :], ya[:, j, :], zx[:, bass.ds(k, 1)], x3[:, j, :],
                                                     ALU.mult, ALU.add).then_inc(v_made, 1)
                            need(dve, v_made, k + 1)
                            need(dve, lap_done, k + 1)
                            dve.scalar_tensor_tensor(x3[:, j, :], wide_of(j, mlp), zy[:, bass.ds(k, 1)], x3[:, j, :],
                                                     ALU.mult, ALU.add).then_inc(x3_made, 1)
                    if mlp and more and t == at["split_xT"]:
                        need(dve, xT_hi_made, s)
                        dve.tensor_tensor(xT_lo, xT_v, xT_hi.bitcast(F32), ALU.subtract).then_inc(xT_lo_made, 1)
                    if front and not mlp and t in EARLY_AT:
                        split_w1_lo(EARLY_AT[t])
                    if first and t in LATE_AT:
                        split_w1_lo(LATE_AT[t])
                    if mlp and experts_at(t, SPLIT_EXPERTS):
                        ahead, c = experts_at(t, SPLIT_EXPERTS)
                        if (ahead and front) or not (ahead or first):
                            split_experts_lo(p + ahead, c)
                for j in range(2 if front else 0):
                    need(dve, x3T_hi_made, 2 * s + j + 1)
                    dve.tensor_tensor(x3T_lo[:, :, j * P:(j + 1) * P], turned[j],
                                      x3T_hi[:, :, j * P:(j + 1) * P].bitcast(F32), ALU.subtract).then_inc(x3T_lo_made, 1)

            setup()
            step(-1, True, False)
            step(0, True, True)
            with nc.vector.Fori(1, NPAIR - 2) as p:
                step(p, True, True)
            step(NPAIR - 2, True, True)
            step(NPAIR - 1, False, True)
            add_residual(NPAIR - 1)

        @block.tensor
        def _(pe):
            def mlp_in(p, t):
                n = HC * p + t
                if isinstance(p, int) and p == 0:
                    pe.wait_ge(w1_lo_made, t + 1)
                if t == 0:
                    need(pe, x3T_hi_made, 2 * (p + 1))
                need(pe, h_lo_made, n - 1)
                products = ((w1_hi, x3T_hi), (w1_lo, x3T_hi), (w1_hi, x3T_lo))
                for i, (w, v) in enumerate(products):
                    if t == 0 and i == 2:
                        need(pe, x3T_lo_made, 2 * (p + 1))
                    for c in range(DC):
                        last = pe.matmul(h_slot(t), w[:, c, t * P:(t + 1) * P], v[:, c, :], start=(c == 0 and i == 0),
                                         stop=(c == DC - 1 and i == 2))
                last.then_inc(h_done, 1)

            def mlp_out(p, t):
                n = HC * p + t
                if isinstance(p, int) and p == 0:
                    pe.wait_ge(w2_lo_made, t + 1)
                elif t % 2 == 0:
                    need(pe, e_lo_made, EPER * (p - 1) + t // 2 + 1)
                need(pe, h_lo_made, n + 1)
                if t == 0:
                    need(pe, sum_made, 4 * p)
                for j in range(2):
                    cols = slice(j * P, j * P + D)
                    for i, (v, w) in enumerate(((h_hi, w2e_hi), (h_hi, w2e_lo), (h_lo, w2e_hi))):
                        last = pe.matmul(acc[j][:, :], v[:, t % 2, j * P:(j + 1) * P], w[:, t, cols],
                                         start=(t == 0 and i == 0), stop=(t == HC - 1 and i == 2))
                    if j == 0 and isinstance(p, int) and p == NPAIR - 1 and t == HC - 1:
                        last.then_inc(acc0_done, 1)
                last.then_inc(out_done, 1)

            def transposes(dst, src, done):
                for c in range(DC):
                    last = pe.transpose(dst[:, c, :], src[:, c * P:(c + 1) * P], ident[:, :])
                last.then_inc(done, 1)

            def split_product(dst, j, v, w, done):
                need(pe, side_hi_made, v + 1)
                need(pe, wide_hi_made[j], w + 1)
                pe.matmul(dst, side_hi[:, :], wide_hi[j], start=True, stop=False)
                need(pe, wide_lo_made[j], w + 1)
                pe.matmul(dst, side_hi[:, :], wide_lo[j], start=False, stop=False)
                need(pe, side_lo_made, v + 1)
                pe.matmul(dst, side_lo[:, :], wide_hi[j], start=False, stop=True).then_inc(done, 1)

            def turn_x3(s, j):
                need(pe, x3_made, 2 * s + j + 1)
                if j == 0:
                    need(pe, x1T_made, 2 * s + 2)
                transposes(turned[j], x3[:, j, :], x3T_done)

            def front_piece(s, t, at, mlp, split):
                if t == at["hid"]:
                    need(pe, th_made, s)
                    if split:
                        need(pe, xT_lo_made, s - 1)
                        need(pe, l0_lo_made, 1)
                        for c in range(DC):
                            for i, (w, v) in enumerate(((l0_w1_hi, xT_hi), (l0_w1_hi, xT_lo), (l0_w1_lo, xT_hi))):
                                last = pe.matmul(sc[:, 0, :], w[:, c, :], v[:, c, :], start=(c == 0 and i == 0),
                                                 stop=(c == DC - 1 and i == 2))
                    else:
                        need(pe, xT_in, 16 * s)
                        for c in range(DC):
                            if not mlp and c % (DC // 2) == 0:
                                pe.wait_ge(hid_in[c // (DC // 2)], 32)
                            last = pe.matmul(sc[:, 0, :], l0_w1_raw[:, c, :], xT_v[:, c, :], start=(c == 0),
                                             stop=(c == DC - 1))
                    last.then_inc(hid_done, 1)
                if t == at["score"]:
                    need(pe, th_made, s + 1)
                    need(pe, ms_made, s)
                    if isinstance(s, int) and s == 0:
                        pe.wait_ge(tab, 5)
                    pe.matmul(sc[:, 1, :], vrep[:, :], th[:, :], start=True, stop=True).then_inc(sc_done, 1)
                for j in range(2):
                    k = 2 * s + j
                    if t == at["pt"][j]:
                        if not mlp:
                            pe.wait_ge(masks_made, MASK_OPS)
                        need(pe, exp_made, k + 1)
                        need(pe, side_lo_made, 4 * s + j)
                        pe.transpose(small[:, 0, :], prob[:, j, :], ident[:, :]).then_inc(pT_done, 1)
                    if t == at["pool"][j]:
                        if j == 0:
                            need(pe, x3T_lo_made, 2 * s)
                        elif mlp:
                            need(pe, x1_made, k)
                        split_product(wide_of(j, mlp), j, 4 * s + j, 3 * s, pool_done)
                    if t == at["turn"][j]:
                        need(pe, x1_made, k + 1)
                        if j == 0:
                            need(pe, x3T_lo_made, 2 * s)
                        else:
                            need(pe, x1T_made, k)
                        transposes(turn, xt[:, j, :], x1T_done)
                    if t == at["down"][j]:
                        need(pe, x1T_made, k + 1)
                        need(pe, dw_in[j], 32 * (s + 1))
                        need(pe, side_lo_made, 4 * s + j + 2)
                        for c in range(DC):
                            last = pe.matmul(small[:, 1, :], adapter(k)[0][:, c, :], x1T_v[:, j, c, :], start=(c == 0),
                                             stop=(c == DC - 1))
                        last.then_inc(down_done, 1)
                    if t == at["up"][j]:
                        if not mlp:
                            need(pe, x1_made, k + 1)
                        elif j == 0:
                            need(pe, x1_made, k + 2)
                        else:
                            need(pe, y_made, k)
                        split_product(wide_of(j, mlp), j, 4 * s + 2 + j, 3 * s + 1, up_done)
                    if t == at["lap"][j]:
                        if not mlp:
                            need(pe, y_made, k + 1)
                        elif j == 0:
                            need(pe, y_made, k + 2)
                        else:
                            need(pe, x3_made, k)
                        need(pe, wide_hi_made[j], 3 * s + 3)
                        pe.matmul(wide_of(j, mlp), lap[:, :], wide_hi[j], start=True, stop=False)
                        need(pe, wide_lo_made[j], 3 * s + 3)
                        pe.matmul(wide_of(j, mlp), lap[:, :], wide_lo[j], start=False, stop=True).then_inc(lap_done, 1)

            def step(p, front, mlp):
                s = p + 1
                at = STEADY if mlp else OPENING
                for t in range(HC if mlp else OPENING_SLOTS):
                    if mlp and t == 0 and not (isinstance(p, int) and p == 0):
                        mlp_out(p - 1, HC - 1)
                    if mlp:
                        mlp_in(p, t)
                    if front:
                        front_piece(s, t, at, mlp, mlp and not (isinstance(p, int) and p == 0))
                    end = front and t == (HC if mlp else OPENING_SLOTS) - 1
                    if end:
                        turn_x3(s, 0)
                    if mlp and t > 0:
                        mlp_out(p, t - 1)
                    if end:
                        turn_x3(s, 1)
                    if t == HC - 1 and isinstance(p, int) and p == 0:
                        pe.wait_ge(w2_lo_made, HC)

            step(-1, True, False)
            step(0, True, True)
            with nc.tensor.Fori(1, NPAIR - 1) as p:
                step(p, True, True)
            step(NPAIR - 1, False, True)
            mlp_out(NPAIR - 1, HC - 1)


TAB_OPS = 19
MASK_OPS = 14


def experts_of(w2e, c):
    return w2e[:, 2 * c:2 * c + 2, :].rearrange("p h (b n) -> p h b n", n=EX)[:, :, 0:5:4, :]


def kernel(**inputs):
    import numpy as np
    import concourse.bacc as bacc
    from concourse.bass_utils import run_bass_kernel_spmd as run

    def row(name):
        return np.ascontiguousarray(inputs[name]).reshape(1, -1)

    def same(name):
        return np.ascontiguousarray(inputs[name])

    x = same("x")
    arrays = {
        "x": x,
        "xT": np.ascontiguousarray(x.reshape(NSEQ * P, D).T),
        "pt": row("itok_B_0_2"), "prof": row("itok_B_0_6"),
        "zXYR": np.concatenate([row("condB_zX"), row("condB_zY"), row("condB_zR")], axis=1),
        "expert": row("itok_B_0_7"),
        "l0_w1": same("L0_cond_W1"),
        "cols": np.ascontiguousarray(np.concatenate([same("L3_cond_b1").reshape(HC, P), row("L0_cond_b1"),
                                                     row("L0_cond_v")]).T),
        "dw": same("L1_cond_down_w"), "db": same("L1_cond_down_b"),
        "uw": same("L1_cond_up_w"), "ub": same("L1_cond_up_b"),
        "lng": same("L1_cond_ln_g"), "lnb": same("L1_cond_ln_b"),
        "w1": same("L3_cond_W1"),
        "w2": same("L3_cond_W2"), "b2": row("L3_cond_b2"),
        "we": same("L3_cond_We"), "be": same("L3_cond_be"),
    }
    nc = bacc.Bacc("TRN2", target_bir_lowering=False, num_devices=1)
    args = [nc.dram_tensor(f"in_{k}", v.shape, mybir.dt.from_np(v.dtype), kind="ExternalInput").ap()
            for k, v in arrays.items()]
    args.append(nc.dram_tensor("out_x", (NSEQ, P, D), F32, kind="ExternalOutput").ap())
    build(nc, *args)
    r = run(nc, [{f"in_{k}": v for k, v in arrays.items()}], core_ids=[0])
    return r.results[0]["out_x"]
```
